# Optimizing a Trainium2 kernel written in Bass

```python
import numpy as np
import jax
import jax.numpy as jnp

def _softmax(x, axis=-1):
    return jax.nn.softmax(x, axis=axis)

def _gelu(x):
    return jax.nn.gelu(x, approximate=True)

def _silu(x):
    return jax.nn.silu(x)

def _sigmoid(x):
    return jax.nn.sigmoid(x)

def _layernorm(x, axis=-1, eps=1e-05):
    m = jnp.mean(x, axis=axis, keepdims=True)
    v = jnp.var(x, axis=axis, keepdims=True)
    return (x - m) / jnp.sqrt(v + eps)

def _scatter_add(tgt, idx, src, axis=0):
    return tgt.at[idx].add(src)

def _segment_sum(src, seg, n):
    return jax.ops.segment_sum(src, seg, n)
kernel_name = 'mk_gnn_resnorm_d4_gnn_r8_94a12a'

def setup_inputs(seed: int=0):
    np.random.seed(seed)
    _w = jnp.asarray

    def _rec_inputs():
        import jax
        import jax.numpy as jnp
        _gk = jax.random.key(seed)
        x = -0.000202 + 1 * jax.random.normal(jax.random.fold_in(_gk, 1), (12500, 128), jnp.float32)
        src = jax.random.randint(jax.random.fold_in(_gk, 2), (200000,), 0, 12500, jnp.int32)
        dst = jnp.minimum((12500 * jax.random.uniform(jax.random.fold_in(_gk, 3), (200000,)) ** 2.0).astype(jnp.int32), 99999)
        _o = jnp.argsort(dst, stable=True)
        src = src[_o]
        dst = dst[_o]
        edge_attr_128 = -4.21973e-05 + 0.999841 * jax.random.normal(jax.random.fold_in(_gk, 12), (200000, 128), jnp.float32)
        return (x, src, dst, edge_attr_128)
    x, src, dst, edge_attr_128 = _rec_inputs()

    def _L0_gnn_setup():
        import jax, jax.numpy as jnp
        import numpy as np
        N_NODES = 6250
        N_EDGES = 200000
        D_IN = 128
        D_OUT = 128
        key = jax.random.key(seed)
        ks = jax.random.split(key, 8)
        feat = jax.random.normal(ks[0], (N_NODES, D_IN), dtype=jnp.float32)
        src = jax.random.randint(ks[1], (N_EDGES,), 0, N_NODES, dtype=jnp.int32)
        dst = jax.random.randint(ks[2], (N_EDGES,), 0, N_NODES, dtype=jnp.int32)
        lim = float(np.sqrt(6.0 / (D_IN + D_OUT))) * float(np.sqrt(2.0))
        W_self = jax.random.uniform(ks[3], (D_OUT, D_IN), jnp.float32, -lim, lim)
        b_self = jnp.zeros((D_OUT,), jnp.float32)
        W_neigh = jax.random.uniform(ks[4], (D_OUT, D_IN), jnp.float32, -lim, lim)
        b_neigh = jnp.zeros((D_OUT,), jnp.float32)
        return {'feat': feat, 'src': src, 'dst': dst, 'W_self': W_self, 'b_self': b_self, 'W_neigh': W_neigh, 'b_neigh': b_neigh}
    _L0_gnn_all = _L0_gnn_setup()
    _L0_gnn_in = {k: v for k, v in _L0_gnn_all.items() if k in ('W_self', 'b_self', 'W_neigh', 'b_neigh')}
    del _L0_gnn_all

    def _L1_gnn_setup():
        import jax, jax.numpy as jnp
        import numpy as np
        N_NODES = 12500
        N_EDGES = 75000
        D_FEAT = 128
        key = jax.random.key(seed)
        k1, k2, k3 = jax.random.split(key, 3)
        x = jax.random.normal(k1, (N_NODES, D_FEAT), dtype=jnp.float32)
        edge_attr = jax.random.normal(k2, (N_EDGES, D_FEAT), dtype=jnp.float32)
        edge_index = jax.random.randint(k3, (2, N_EDGES), 0, N_NODES, dtype=jnp.int64)
        return {'x': x, 'edge_attr': edge_attr, 'edge_index': edge_index}
    _L1_gnn_all = _L1_gnn_setup()
    _L1_gnn_in = {k: v for k, v in _L1_gnn_all.items() if k in ()}
    del _L1_gnn_all

    def _L2_gnn_setup():
        import jax, jax.numpy as jnp
        import numpy as np
        N = 6250
        E = 200000
        INPUT_DIM = 128
        HEADS = 4
        OUT_DIM = 32
        LRELU_ALPHA = 0.2
        key = jax.random.key(seed)
        k1, k2, k3, k4, k5 = jax.random.split(key, 5)
        gain = 1.0 / (1.0 + LRELU_ALPHA)
        input_proj = jax.random.normal(k1, (N, INPUT_DIM), dtype=jnp.float32)
        edge_index = jax.random.randint(k2, (2, E), 0, N, dtype=jnp.int64)
        W = jax.random.normal(k3, (INPUT_DIM, HEADS * OUT_DIM), dtype=jnp.float32) * (gain / INPUT_DIM) ** 0.5
        A_left = jax.random.normal(k4, (HEADS, OUT_DIM, 1), dtype=jnp.float32) * (gain / OUT_DIM)
        A_right = jax.random.normal(k5, (HEADS, OUT_DIM, 1), dtype=jnp.float32) * (gain / OUT_DIM)
        return {'input_proj': input_proj, 'edge_index': edge_index, 'W': W, 'A_left': A_left, 'A_right': A_right}
    _L2_gnn_all = _L2_gnn_setup()
    _L2_gnn_in = {k: v for k, v in _L2_gnn_all.items() if k in ('W', 'A_left', 'A_right')}
    del _L2_gnn_all

    def _L3_gnn_setup():
        import jax, jax.numpy as jnp
        import numpy as np
        N = 12500
        E_RAND = 400000
        F_IN = 128
        D = 64
        SUBHEADS = 2
        ALPHA = 0.2
        key = jax.random.key(seed)
        ks = jax.random.split(key, 8)
        x = jax.random.normal(ks[0], (N, F_IN), jnp.float32)
        src = jax.random.randint(ks[1], (E_RAND,), 0, N)
        dst = jax.random.randint(ks[2], (E_RAND,), 0, N)
        loops = jnp.arange(N)
        edge_index = jnp.stack([jnp.concatenate([src, loops]), jnp.concatenate([dst, loops])])
        xav = lambda k, shp, fan: jax.random.normal(k, shp, jnp.float32) * np.float32(1.414 * np.sqrt(2.0 / fan))
        W = xav(ks[3], (SUBHEADS, F_IN, D), F_IN + D)
        b = jnp.zeros((SUBHEADS, D), jnp.float32)
        fc = xav(ks[4], (SUBHEADS, D, 1), D + 1)
        bf = jnp.zeros((SUBHEADS,), jnp.float32)
        a_src = xav(ks[5], (SUBHEADS, D), D + 1)
        a_dst = xav(ks[6], (SUBHEADS, D), D + 1)
        return dict(x=x, edge_index=edge_index, W=W, b=b, fc=fc, bf=bf, a_src=a_src, a_dst=a_dst)
    _L3_gnn_all = _L3_gnn_setup()
    _L3_gnn_in = {k: v for k, v in _L3_gnn_all.items() if k in ('W', 'b', 'fc', 'bf', 'a_src', 'a_dst')}
    del _L3_gnn_all
    return {'x': x, 'src': src, 'dst': dst, 'edge_attr_128': edge_attr_128, 'L0_gnn_W_self': _L0_gnn_in['W_self'], 'L0_gnn_b_self': _L0_gnn_in['b_self'], 'L0_gnn_W_neigh': _L0_gnn_in['W_neigh'], 'L0_gnn_b_neigh': _L0_gnn_in['b_neigh'], 'L2_gnn_W': _L2_gnn_in['W'], 'L2_gnn_A_left': _L2_gnn_in['A_left'], 'L2_gnn_A_right': _L2_gnn_in['A_right'], 'L3_gnn_W': _L3_gnn_in['W'], 'L3_gnn_b': _L3_gnn_in['b'], 'L3_gnn_fc': _L3_gnn_in['fc'], 'L3_gnn_bf': _L3_gnn_in['bf'], 'L3_gnn_a_src': _L3_gnn_in['a_src'], 'L3_gnn_a_dst': _L3_gnn_in['a_dst']}

def reference(x, src, dst, edge_attr_128, L0_gnn_W_self, L0_gnn_b_self, L0_gnn_W_neigh, L0_gnn_b_neigh, L2_gnn_W, L2_gnn_A_left, L2_gnn_A_right, L3_gnn_W, L3_gnn_b, L3_gnn_fc, L3_gnn_bf, L3_gnn_a_src, L3_gnn_a_dst):
    import jax
    import jax.numpy as jnp

    def _L0_gnn_ref(feat, src, dst, W_self, b_self, W_neigh, b_neigh):
        import jax, jax.numpy as jnp
        import numpy as np
        N_NODES = 6250
        N_EDGES = 200000
        D_IN = 128
        D_OUT = 128
        "GraphSAGE 'mean' aggregator, eval mode (feat_drop=0).\n\n            in_feats == out_feats -> lin_before_mp is False:\n              h_neigh = fc_neigh(mean_{u in N(v)} feat[u])\n              rst     = fc_self(feat[v]) + h_neigh\n            Zero in-degree nodes get a zero neighbor vector (DGL mean semantics).\n            "
        n = feat.shape[0]
        msg = feat[src]
        agg = jax.ops.segment_sum(msg, dst, num_segments=n)
        deg = jax.ops.segment_sum(jnp.ones_like(src, feat.dtype), dst, num_segments=n)
        h_neigh = agg / jnp.maximum(deg, 1.0)[:, None]
        h_neigh = h_neigh @ W_neigh.T + b_neigh
        h_self = feat @ W_self.T + b_self
        return h_self + h_neigh

    def _L1_gnn_ref(x, edge_attr, edge_index):
        import jax, jax.numpy as jnp
        import numpy as np
        N_NODES = 12500
        N_EDGES = 75000
        D_FEAT = 128
        src, dst = (edge_index[0], edge_index[1])
        x_src = x[src]
        messages = x_src + edge_attr
        aggr = jax.ops.segment_sum(messages, dst, num_segments=x.shape[0])
        return x + aggr

    def _L2_gnn_ref(input_proj, edge_index, W, A_left, A_right):
        import jax, jax.numpy as jnp
        import numpy as np
        N = 6250
        E = 200000
        INPUT_DIM = 128
        HEADS = 4
        OUT_DIM = 32
        LRELU_ALPHA = 0.2
        n = input_proj.shape[0]
        heads, out_dim = (A_left.shape[0], A_left.shape[1])
        H = (input_proj @ W).reshape(n, heads, out_dim)
        H_s = jnp.einsum('nhd,hd->nh', H, A_left[..., 0])
        H_t = jnp.einsum('nhd,hd->nh', H, A_right[..., 0])
        src = edge_index[0]
        tgt = edge_index[1]
        e = H_s[src] + H_t[tgt]
        e = jnp.where(e > 0, e, LRELU_ALPHA * e)
        e = jnp.exp(e - jnp.max(e))
        denom = jax.ops.segment_sum(e, src, num_segments=n)
        alpha = e / (denom[src] + 1e-08)
        msg = alpha[:, :, None] * H[tgt]
        agg = jax.ops.segment_sum(msg, src, num_segments=n)
        res = agg.reshape(n, heads * out_dim)
        return jax.nn.elu(res)

    def _L3_gnn_ref(x, edge_index, W, b, fc, bf, a_src, a_dst):
        import jax, jax.numpy as jnp
        import numpy as np
        N = 12500
        E_RAND = 400000
        F_IN = 128
        D = 64
        SUBHEADS = 2
        ALPHA = 0.2
        row, col = (edge_index[0], edge_index[1])
        n = x.shape[0]
        outs = []
        for i in range(SUBHEADS):
            h = x @ W[i]
            s_r = h @ a_src[i]
            s_c = h @ a_dst[i]
            e = jax.nn.leaky_relu(s_r[row] + s_c[col], ALPHA)
            m = jax.ops.segment_max(e, row, num_segments=n)
            ee = jnp.exp(e - m[row])
            denom = jax.ops.segment_sum(ee, row, num_segments=n)
            att = ee / denom[row]
            rs = jax.ops.segment_sum(att, row, num_segments=n)
            val = att / jnp.where(rs == 0, 1.0, rs)[row]
            vh = h
            for _ in range(i + 1):
                vh = jax.ops.segment_sum(val[:, None] * vh[col], row, num_segments=n)
            vh = jnp.where(jnp.isnan(vh), 0.0, vh)
            vh = vh + b[i]
            g = jax.nn.sigmoid(vh @ fc[i] + bf[i])
            vh = jnp.maximum(vh, 0.0) + g * jnp.minimum(vh, 0.0)
            vh = jax.nn.leaky_relu(vh, ALPHA)
            outs.append(vh)
        return jnp.concatenate(outs, axis=1)
    edge_index = jnp.stack([src, dst])
    x = _layernorm(x + _L0_gnn_ref(x, src, dst, L0_gnn_W_self, L0_gnn_b_self, L0_gnn_W_neigh, L0_gnn_b_neigh), axis=-1)
    x = _layernorm(x + _L1_gnn_ref(x, edge_attr_128, edge_index), axis=-1)
    x = _layernorm(x + _L2_gnn_ref(x, edge_index, L2_gnn_W, L2_gnn_A_left, L2_gnn_A_right), axis=-1)
    x = _layernorm(x + _L3_gnn_ref(x, edge_index, L3_gnn_W, L3_gnn_b, L3_gnn_fc, L3_gnn_bf, L3_gnn_a_src, L3_gnn_a_dst), axis=-1)
    return x

_drawn_inputs = setup_inputs


def setup_inputs(seed=0):
    import zlib

    import numpy as np

    out = dict(_drawn_inputs(seed))
    spreads = {'L0_gnn_b_self': (0.0, 0.1),
     'L0_gnn_b_neigh': (0.0, 0.1),
     'L3_gnn_b': (0.0, 0.1),
     'L3_gnn_bf': (0.0, 0.1)}
    factors = {}
    for name, (base, spread) in spreads.items():
        noise = np.random.default_rng([zlib.crc32(name.encode()), seed]).standard_normal(out[name].shape)
        drawn = base * np.exp(spread * noise) if base else spread * noise
        out[name] = jnp.asarray(drawn.astype(out[name].dtype))
    for name, factor in factors.items():
        out[name] = (out[name] * factor).astype(out[name].dtype)
    return out
```

```python
from contextlib import ExitStack

import concourse.bass as bass
from concourse import mybir
from concourse.alu_op_type import AluOpType as ALU

ACT = mybir.ActivationFunctionType
F32 = mybir.dt.float32
I32 = mybir.dt.int32
AX = mybir.AxisListType.X
RMAX = bass.bass_isa.ReduceOp.max

P = 128
D = 128
N = 12500
E = 200000
NB = -(-N // P)
LAST = N - (NB - 1) * P
EP = 125
EC = E // EP
G = 4
T = -(-((E + NB * (P - 1)) // P) // (2 * G)) * (2 * G)
NG = T // G
TX = T + G
CB = 7
NC = NB // CB
RW = 132
NO_NODE = 255
EPS = 1e-5
SLOPE = 0.2


class Parts:
    pass


def take(eng, sem, n=1):
    eng.wait_ge(sem, n).then_inc(sem, -n)


def bc(ap, shape):
    return ap.broadcast_to(list(shape))


def build(nc, a, out):
    with ExitStack() as ctx:
        def sb(name, shape, dt=F32):
            return ctx.enter_context(nc.sbuf_tensor(name, shape, dt))

        m = Parts()
        m.nc, m.a, m.out = nc, a, out
        m.sem = lambda name: ctx.enter_context(nc.semaphore(name))
        tokens = {}

        def token(name):
            if name not in tokens:
                tokens[name] = m.sem(name)
            return tokens[name]
        m.token = token

        def dram(name, shape, dt=F32):
            return nc.dram_tensor(name, shape, dt).ap()
        m.rec_dst = dram("rec_by_dst", (P * T, 4), I32)
        m.rec_src = dram("rec_by_src", (P * T, 4), I32)
        m.tab1 = dram("x1_rows", (NB * P, D))
        m.tab2 = dram("h2_rows", (NB * P, RW))
        m.tab3 = dram("h3_rows", (NB * P, D + 2))
        m.tab4 = dram("hop_rows", (NB * P, 64))

        m.X = sb("X", [P, NB, D])
        m.A = sb("A", [P, NB, RW])
        m.gi_d, m.gi_s = sb("gi_d", [P, TX], I32), sb("gi_s", [P, TX], I32)
        m.ei_d = sb("ei_d", [P, TX], I32)
        m.li_d, m.li_s = sb("li_d", [P, TX]), sb("li_s", [P, TX])
        m.neg = sb("neg", [P, TX])
        m.w1 = m.ei_d[:].bitcast(F32)
        m.bt_d, m.bt_s = sb("bt_d", [1, TX], I32), sb("bt_s", [1, TX], I32)
        m.ring = sb("ring", [P, 2, G, RW])
        m.ring2 = sb("ring2", [P, 2, G, D])
        m.idx = sb("idx", [P, 2, 2 * G], I32)
        m.oh = sb("oh", [P, 2, G, P])
        m.ohT = sb("ohT", [P, 2, G, P])
        m.sc = sb("sc", [P, 2, G, 4])
        m.lr = sb("lr", [P, 2, G, 4])
        m.dd = sb("dd", [P, 2, G, 4])
        m.rmax = sb("rmax", [P, G, 4])
        m.gmax = sb("gmax", [P, 4])
        m.node = sb("node", [P, NB, 8])
        m.nbr = sb("nbr", [P, NB, 4])
        m.rec = sb("rec", [P, NB, 4])
        m.tmp4 = sb("tmp4", [P, NB, 4])
        m.iota = sb("iota", [P, P])
        m.pidx = sb("pidx", [P, 1])
        m.ident = sb("ident", [P, P])
        m.tri = sb("tri", [P, P])
        m.ones = sb("ones", [P, P])
        m.iota_b = sb("iota_b", [P, NB])
        m.w = {n: sb("w_" + n, [P, D]) for n in ("self", "neigh", "l2", "l3", "t1", "b3", "fc3")}
        m.wa2, m.wa3 = sb("wa2", [P, 8]), sb("wa3", [P, 4])
        m.bd = sb("bd", [P, 12])
        m.bias = sb("bias", [1, 2, D])
        m.bf3 = sb("bf3", [P, 2])
        m.Y = sb("Y", [P, CB, D])
        m.S = sb("S", [P, CB, D])
        ring_view = lambda t: t[:].rearrange("p h j n -> p (h j) n")[:, 0:CB, :]
        m.M, m.xT, m.mT = ring_view(m.oh), ring_view(m.ohT), ring_view(m.ring2)
        m.HR = sb("HR", [P, CB, RW])
        m.st = sb("st", [P, 4, CB])
        m.gg = sb("gg", [P, CB, 2])
        m.PS = ctx.enter_context(nc.psum_tensor("PS", [P, 8, 512], F32))

        prepare(m)
        group_edges(m, "d", a["dst"], a["src"], m.rec_dst, m.gi_d, m.li_d, m.ei_d, m.bt_d)
        group_edges(m, "s", a["src"], a["dst"], m.rec_src, m.gi_s, m.li_s, None, m.bt_s)
        load_nodes(m)
        edge_pass(m, "e0", a["x"], D, m.gi_d, m.li_d, m.bt_d, 0, D + 1, ones=True)
        nodes_sage(m)
        edge_pass(m, "e1", m.tab1, D, m.gi_d, m.li_d, m.bt_d, 0, D, attr=True)
        nodes_project(m, "n1", m.w["l2"], m.wa2, 4, m.tab2, D + 4, after_attention=False)
        edge_pass(m, "e2", m.tab2, D + 4, m.gi_s, m.li_s, m.bt_s, 0, D + 4, heads=4)
        nodes_project(m, "n2", m.w["l3"], m.wa3, 2, m.tab3, D + 2, after_attention=True)
        edge_pass(m, "e3", m.tab3, D + 2, m.gi_s, m.li_s, m.bt_s, 0, D + 2, heads=2)
        nodes_hop(m)
        edge_pass(m, "e4", m.tab4, 64, m.gi_s, m.li_s, m.bt_s, 64, 64, weights=m.w1)
        nodes_final(m)


def prepare(m):
    nc, a = m.nc, m.a
    loaded, made, step = m.sem("w_loaded"), m.sem("const_made"), m.sem("w_step")
    pe_done, copied, zeroed = m.sem("w_pe"), m.sem("w_copied"), m.sem("w_zeroed")
    n_loads = 10 + 8 + 4
    with nc.Block() as block:
        @block.sync
        def _(sp):
            sp.dma_start(m.w["self"][:], a["L0_gnn_W_self"]).then_inc(loaded, 16)
            sp.dma_start(m.w["neigh"][:], a["L0_gnn_W_neigh"]).then_inc(loaded, 16)
            sp.dma_start(m.w["l2"][:], a["L2_gnn_W"]).then_inc(loaded, 16)
            for i in range(2):
                sp.dma_start(m.w["l3"][:, 64 * i:64 * i + 64], a["L3_gnn_W"][i]).then_inc(loaded, 16)
            sp.dma_start(m.bias[:, 0, :], a["L0_gnn_b_self"].rearrange("(o d) -> o d", o=1)).then_inc(loaded, 16)
            sp.dma_start(m.bias[:, 1, :], a["L0_gnn_b_neigh"].rearrange("(o d) -> o d", o=1)).then_inc(loaded, 16)
            sp.dma_start(m.w["b3"][:], a["L3_gnn_b"].rearrange("i d -> (i d)").partition_broadcast(P)).then_inc(loaded, 16)
            sp.dma_start(m.w["fc3"][:], a["L3_gnn_fc"].rearrange("i d o -> (i d o)").partition_broadcast(P)).then_inc(loaded, 16)
            sp.dma_start(m.bf3[:], a["L3_gnn_bf"].partition_broadcast(P)).then_inc(loaded, 16)
            sp.wait_ge(zeroed, 1)
            for h in range(4):
                sp.dma_start(m.bd[32 * h:32 * h + 32, h:h + 1], a["L2_gnn_A_right"][h]).then_inc(loaded, 16)
                sp.dma_start(m.bd[32 * h:32 * h + 32, 4 + h:5 + h], a["L2_gnn_A_left"][h]).then_inc(loaded, 16)
            for i in range(2):
                for col, name in ((8, "L3_gnn_a_dst"), (10, "L3_gnn_a_src")):
                    sp.dma_start(m.bd[64 * i:64 * i + 64, col + i:col + i + 1],
                                 a[name][i].rearrange("(d o) -> d o", o=1)).then_inc(loaded, 16)

        @block.gpsimd
        def _(pool):
            kw = dict(allow_small_or_imprecise_dtypes=True)
            nc.gpsimd.iota(m.iota[:], [[1, P]], base=0, channel_multiplier=0, **kw).then_inc(made, 1)
            nc.gpsimd.iota(m.pidx[:], [[0, 1]], base=0, channel_multiplier=1, **kw).then_inc(made, 1)
            nc.gpsimd.iota(m.iota_b[:], [[1, NB]], base=0, channel_multiplier=0, **kw).then_inc(made, 1)
            nc.gpsimd.memset(m.ones[:], 1.0).then_inc(made, 1)

        @block.vector
        def _(v):
            nc.vector.memset(m.bd[:], 0.0).then_inc(zeroed, 1)
            v.wait_ge(made, 4)
            nc.vector.tensor_scalar(m.ident[:], m.iota[:], m.pidx[:], None, ALU.is_equal).then_inc(step, 1)
            nc.vector.tensor_scalar(m.tri[:], m.iota[:], m.pidx[:], None, ALU.is_gt).then_inc(step, 1)
            v.wait_ge(loaded, 16 * n_loads)
            v.wait_ge(pe_done, 1)
            nc.vector.tensor_copy(m.w["self"][:], m.PS[:, 0, 0:D]).then_inc(copied, 1)
            nc.vector.tensor_copy(m.w["neigh"][:], m.PS[:, 1, 0:D]).then_inc(copied, 1)
            nc.vector.tensor_copy(m.w["t1"][:], m.PS[:, 2, 0:D]).then_inc(copied, 1)
            nc.vector.tensor_copy(m.M[:, 0, :], m.PS[:, 3, 0:D]).then_inc(copied, 1)
            v.wait_ge(pe_done, 2)
            nc.vector.tensor_copy(m.wa2[:], m.PS[:, 4, 0:8]).then_inc(copied, 1)
            nc.vector.tensor_copy(m.wa3[:], m.PS[:, 5, 0:4]).then_inc(copied, 1)

        @block.tensor
        def _(pe):
            pe.wait_ge(loaded, 16 * n_loads)
            pe.wait_ge(step, 2)
            for k, name in enumerate(("self", "neigh", "l2", "l3")):
                t = nc.tensor.transpose(m.PS[:, k, 0:D], m.w[name][:], m.ident[:])
            t.then_inc(pe_done, 1)
            pe.wait_ge(copied, 4)
            nc.tensor.matmul(m.PS[:, 4, 0:8], m.w["t1"][:], m.bd[:, 0:8], start=True, stop=True)
            nc.tensor.matmul(m.PS[:, 5, 0:4], m.M[:, 0, :], m.bd[:, 8:12], start=True, stop=True).then_inc(pe_done, 1)


def group_edges(m, tag, key, other, rec, gi, li, ei, bt):
    nc = m.nc
    A = m.A[:].rearrange("p b w -> p (b w)")
    Xf = m.X[:].rearrange("p b w -> p (b w)")
    AI, XI = A.bitcast(I32), Xf.bitcast(I32)
    recs = AI[0:EP, 0:4 * EC].rearrange("p (c w) -> p c w", w=4)
    k_i = AI[0:EP, 4 * EC:5 * EC]
    blk = A[0:EP, 5 * EC:6 * EC]
    mask = AI[0:EP, 6 * EC:7 * EC]
    run = A[0:EP, 7 * EC:8 * EC]
    pos = Xf[0:EP, 0:EC]
    row = XI[0:EP, EC:2 * EC]
    oth = XI[0:EP, 2 * EC:3 * EC]
    hi = XI[0:EP, 3 * EC:4 * EC]
    zero = Xf[0:EP, 4 * EC:5 * EC]
    fill = XI[:, 5 * EC:5 * EC + 2 * G * 4].rearrange("p (t w) -> p t w", w=4)
    small = Xf[:, 5 * EC + 64:5 * EC + 64 + 6 * NB].rearrange("p (k b) -> p k b", b=NB)
    smalli = XI[:, 5 * EC + 64 + 6 * NB:5 * EC + 64 + 7 * NB]
    icol = Xf[0:NB, 5 * EC + 64 + 7 * NB:5 * EC + 65 + 7 * NB]
    cnt, tiles, incl, base = (small[:, k, :] for k in range(4))
    iota_t = Xf[0:NB, 9000:9000 + TX]
    cmp = Xf[0:NB, 10680:10680 + TX]
    back = AI[:, 0:4 * T].rearrange("p (t w) -> p t w", w=4)
    slots = m.idx[0:EP]
    rring = m.ring2[:].bitcast(I32)

    loaded, filled, fill_out = (m.sem(tag + x) for x in ("_loaded", "_fill", "_fill_out"))
    ch, cnt_ok, psum_ok, col_ok, cmp_ok, bt_ok, pos_ok = (
        m.sem(tag + x) for x in ("_ch", "_cnt", "_psum", "_col", "_cmp", "_bt", "_pos"))
    ring_ok, scattered, seen, back_ok, io = (m.sem(tag + "_ring"), [m.sem(f"{tag}_sc{h}") for h in range(2)],
                                             m.sem(tag + "_seen"), m.sem(tag + "_back"), m.sem(tag + "_iota"))
    NGE = EC // G
    with nc.Block() as block:
        @block.sync
        def _(sp):
            sp.dma_start(k_i, key.rearrange("(p c) -> p c", c=EC)).then_inc(loaded, 16)
            sp.dma_start(oth, other.rearrange("(p c) -> p c", c=EC)).then_inc(loaded, 16)
            sp.wait_ge(filled, 1)
            r = rec.rearrange("(p t) w -> p t w", p=P)
            for c in range(T // (2 * G)):
                sp.dma_start(r[:, 2 * G * c:2 * G * (c + 1), :], fill).then_inc(fill_out, 16)
            for h in range(2):
                sp.wait_ge(scattered[h], 16 * G)
                sp.sem_inc(seen)
            with sp.Fori(1, NGE // 2) as i:
                for h in range(2):
                    sp.wait_ge(scattered[h], 16 * G * (i + 1))
                    sp.sem_inc(seen)
            sp.dma_start(back, rec.rearrange("(p t) w -> p t w", p=P)).then_inc(back_ok, 16)

        @block.gpsimd
        def _(pool):
            nc.gpsimd.iota(iota_t, [[1, TX]], base=0, channel_multiplier=0,
                           allow_small_or_imprecise_dtypes=True).then_inc(io, 1)
            pool.wait_ge(fill_out, 16 * (T // (2 * G)))
            with pool.Fori(0, NGE // 2) as i:
                for h in range(2):
                    take(pool, ring_ok)
                    for j in range(G):
                        nc.gpsimd.indirect_dma_start(
                            out=rec, out_offset=bass.IndirectOffsetOnAxis(ap=slots[:, h, j:j + 1], axis=0),
                            in_=rring[0:EP, h, j, 0:4], in_offset=None).then_inc(scattered[h], 16)

        @block.scalar
        def _(act):
            act.wait_ge(pos_ok, 1)

            def fill_ring(g, h):
                nc.scalar.copy(slots[:, h, 0:G], row[:, bass.ds(g * G, G)])
                nc.scalar.copy(rring[0:EP, h, :, 0:4], recs[:, bass.ds(g * G, G), :]).then_inc(ring_ok, 1)
            fill_ring(0, 0)
            fill_ring(1, 1)
            with act.Fori(1, NGE // 2) as i:
                for h in range(2):
                    take(act, seen)
                    fill_ring(2 * i + h, h)

        @block.tensor
        def _(pe):
            pe.wait_ge(cnt_ok, 1)
            nc.tensor.matmul(m.PS[:, 0, 0:NB], m.ones[0:EP, :], cnt[0:EP, :], start=True, stop=True)
            nc.tensor.matmul(m.PS[:, 1, 0:NB], m.tri[0:EP, :], cnt[0:EP, :], start=True, stop=True).then_inc(psum_ok, 1)
            pe.wait_ge(col_ok, 1)
            nc.tensor.transpose(m.PS[0:NB, 2, 0:P], incl, m.ident[:]).then_inc(psum_ok, 1)
            pe.wait_ge(cmp_ok, 1)
            q = TX // 4
            for k in range(4):
                t = nc.tensor.matmul(m.PS[0:1, 3 + k, 0:q], m.ones[0:NB, 0:1], cmp[:, q * k:q * k + q],
                                     start=True, stop=True)
            t.then_inc(bt_ok, 1)

        @block.vector
        def _(v):
            def seq(ins):
                ins.then_inc(ch, 1)
                take(v, ch)
            V = nc.vector
            V.memset(fill, 0)
            seq(V.memset(zero, 0.0))
            V.memset(fill[:, :, 1:2], NO_NODE).then_inc(filled, 1)
            seq(V.memset(cnt, 0.0))
            seq(V.memset(pos, 0.0))
            v.wait_ge(loaded, 32)
            seq(V.tensor_scalar(hi, k_i, 7, None, ALU.logical_shift_right))
            seq(V.tensor_copy(blk, hi))
            seq(V.tensor_copy(recs[:, :, 0], oth))
            seq(V.tensor_scalar(recs[:, :, 1], k_i, P - 1, None, ALU.bitwise_and))
            seq(V.tensor_scalar(run, zero, 1.0, None, ALU.add))
            seq(V.tensor_tensor_scan(pos, run, zero, -1.0, ALU.add, ALU.add))
            seq(V.tensor_scalar(small[0:EP, 5, 0:1], m.pidx[0:EP, :], float(EC), None, ALU.mult))
            seq(V.tensor_scalar(recs[:, :, 2], pos, small[0:EP, 5, 0:1], None, ALU.add))
            seq(V.tensor_copy(recs[:, :, 3], zero))
            with v.Fori(0, NB) as b:
                seq(V.tensor_scalar(run, blk, m.iota_b[0:EP, bass.ds(b, 1)], None, ALU.is_equal, ALU.add,
                                    accum_out=cnt[0:EP, bass.ds(b, 1)]))
            V.memset(small[:, 4, :], 0.0).then_inc(cnt_ok, 1)
            v.wait_ge(psum_ok, 1)
            seq(V.tensor_scalar(tiles, m.PS[:, 0, 0:NB], float(P - 1), None, ALU.add))
            seq(V.tensor_copy(smalli, tiles))
            seq(V.tensor_scalar(smalli, smalli, 7, None, ALU.logical_shift_right))
            seq(V.tensor_copy(tiles, smalli))
            seq(V.tensor_tensor_scan(incl, tiles, small[:, 4, :], 0.0, ALU.add, ALU.add))
            seq(V.tensor_tensor(base, incl, tiles, ALU.subtract))
            seq(V.tensor_scalar(base, base, float(P), -1.0, ALU.mult, ALU.add))
            seq(V.tensor_tensor(base, base, m.PS[:, 1, 0:NB], ALU.add))
            V.memset(small[:, 5, :], 0.0).then_inc(col_ok, 1)
            v.wait_ge(psum_ok, 2)
            v.wait_ge(io, 1)
            seq(V.tensor_copy(icol, m.PS[0:NB, 2, 0:1]))
            V.tensor_scalar(cmp, iota_t, icol, None, ALU.is_ge).then_inc(cmp_ok, 1)
            v.wait_ge(bt_ok, 1)
            q = TX // 4
            for k in range(4):
                seq(V.tensor_scalar(bt[:, q * k:q * k + q], m.PS[0:1, 3 + k, 0:q], float(NB - 1), None, ALU.min))
            with v.Fori(0, NB) as b:
                seq(V.tensor_scalar(mask, blk, m.iota_b[0:EP, bass.ds(b, 1)], None, ALU.is_equal))
                seq(V.tensor_copy(small[0:EP, 5, 0:1], base[0:EP, bass.ds(b, 1)]))
                seq(V.tensor_tensor_scan(run, mask, zero, small[0:EP, 5, 0:1], ALU.add, ALU.add))
                seq(V.copy_predicated(pos, mask, run))
            seq(V.tensor_copy(row, pos))
            seq(V.tensor_scalar(hi, row, 7, None, ALU.logical_shift_right))
            seq(V.tensor_scalar(row, row, P - 1, None, ALU.bitwise_and))
            V.scalar_tensor_tensor(out=row, in0=row, scalar=float(T), in1=hi, op0=ALU.mult, op1=ALU.add).then_inc(pos_ok, 1)
            V.memset(gi[:, T:TX], 0)
            V.memset(li[:, T:TX], float(NO_NODE))
            if ei is not None:
                V.memset(ei[:, T:TX], 0)
            v.wait_ge(back_ok, 16)
            V.tensor_copy(gi[:, 0:T], back[:, :, 0])
            seq(V.tensor_copy(li[:, 0:T], back[:, :, 1]))
            if ei is not None:
                V.tensor_copy(ei[:, 0:T], back[:, :, 2])
            else:
                V.tensor_scalar(m.neg[:], li[:], float(NO_NODE), -1e30, ALU.is_equal, ALU.mult)


def load_nodes(m):
    nc = m.nc
    z, ld = m.sem("x_zero"), m.sem("x_loaded")
    with nc.Block() as block:
        @block.vector
        def _(v):
            nc.vector.memset(m.X[:, NB - 1, :], 0.0).then_inc(z, 1)

        @block.sync
        def _(sp):
            full = (NB - 1) * P
            sp.dma_start(m.X[:, 0:NB - 1, :], m.a["x"][0:full, :].rearrange("(b p) d -> p b d", p=P)).then_inc(ld, 16)
            sp.wait_ge(z, 1)
            sp.dma_start(m.X[0:LAST, NB - 1, :], m.a["x"][full:N, :]).then_inc(ld, 16)
            sp.wait_ge(ld, 32)


def edge_pass(m, tag, table, width, gi, li, bt, col, ncols, ones=False, attr=False, heads=0, weights=None):
    nc = m.nc
    per = 2 * G if attr else G
    got = [m.sem(f"{tag}_got{h}") for h in range(2)]
    s = Parts()
    s.idx_ready = m.token("idx_ready")
    s.idx_free = m.token("idx_free")
    s.ring_free = m.token("ring_free")
    s.landed = m.token("landed")
    s.oh_ready = m.token("oh_ready")
    s.summed = m.token("summed")
    s.ps_free = m.token("ps_free")
    s.added = m.token("added")
    s.ohT_psum = m.token("ohT_psum")
    s.ohT_ready = m.token("ohT_ready")
    s.hs_ready = m.token("hs_ready")
    s.d_ready = m.token("d_ready")
    s.w_ready = m.token("w_ready")
    s.msg_ready = m.token("msg_ready")
    s.ch = m.token("ch")
    s.init = m.token("init")
    PM = lambda h, j: m.PS[:, 2 * h + j // 2, RW * (j % 2):RW * (j % 2) + ncols]
    PT = lambda h: m.PS[:, 4 + h, :].rearrange("p (j n) -> p j n", j=G)
    PH = lambda h: m.PS[:, 6 + h, 0:8 * G].rearrange("p (j n) -> p j n", j=G)
    nh = heads

    def groups(eng, body):
        body(0, 0, 0, True)
        body(1, 1, 0, True)
        with eng.Fori(1, NG // 2) as i:
            for h in range(2):
                body(2 * i + h, h, i, False)

    with nc.Block() as block:
        @block.sync
        def _(sp):
            def body(g, h, i, peeled):
                sp.wait_ge(got[h], 16 * per * (i + 1))
                sp.sem_inc(s.idx_free)
                sp.sem_inc(s.landed)
            groups(sp, body)

        @block.gpsimd
        def _(pool):
            def body(g, h, i, peeled):
                take(pool, s.idx_ready)
                if not peeled:
                    take(pool, s.ring_free)
                for j in range(G):
                    nc.gpsimd.indirect_dma_start(
                        out=m.ring[:, h, j, 0:width], out_offset=None, in_=table,
                        in_offset=bass.IndirectOffsetOnAxis(ap=m.idx[:, h, j:j + 1], axis=0)).then_inc(got[h], 16)
                    if attr:
                        nc.gpsimd.indirect_dma_start(
                            out=m.ring2[:, h, j, :], out_offset=None, in_=m.a["edge_attr_128"],
                            in_offset=bass.IndirectOffsetOnAxis(ap=m.idx[:, h, G + j:G + j + 1], axis=0)
                        ).then_inc(got[h], 16)
            groups(pool, body)
            take(pool, s.ring_free)

        @block.scalar
        def _(act):
            def indices(g, h, sem=True):
                ins = nc.scalar.copy(m.idx[:, h, 0:G], gi[:, bass.ds(g * G, G)])
                if attr:
                    ins = nc.scalar.copy(m.idx[:, h, G:2 * G], m.ei_d[:, bass.ds(g * G, G)])
                ins.then_inc(s.idx_ready, 1)

            def transposed(h):
                take(act, s.ohT_psum)
                nc.scalar.copy(m.ohT[:, h], PT(h)).then_inc(s.ohT_ready, 1)

            indices(0, 0)
            indices(1, 1)
            if nh:
                transposed(0)

            def body(g, h, i, peeled):
                if nh:
                    transposed(1 - h)
                    take(act, s.d_ready)
                    nc.scalar.activation(m.ring[:, h, :, D:D + nh], m.dd[:, h, :, 0:nh], ACT.Exp).then_inc(s.w_ready, 1)
                    if nh == 2:
                        nc.scalar.activation(m.w1[:, bass.ds(g * G, G)], m.dd[:, h, :, 1], ACT.Exp)

            def last(g, h, i, peeled):
                body(g, h, i, peeled)
                take(act, s.idx_free)
                indices(g + 2, h)
            last(0, 0, 0, True)
            last(1, 1, 0, True)
            with act.Fori(1, NG // 2 - 1) as i:
                for h in range(2):
                    last(2 * i + h, h, i, False)
            body(NG - 2, 0, 0, False)
            body(NG - 1, 1, 0, False)
            take(act, s.idx_free, 2)

        @block.tensor
        def _(pe):
            take(pe, s.init)

            def scores(g, h):
                take(pe, s.oh_ready)
                for j in range(G):
                    t = nc.tensor.transpose(PT(h)[:, j, :], m.oh[:, h, j, :], m.ident[:])
                t.then_inc(s.ohT_psum, 1)
                blocks = [pe.value_load(bt[0:1, bass.ds(g * G + j, 1)], min_val=0, max_val=NB - 1) for j in range(G)]
                take(pe, s.ohT_ready)
                for j in range(G):
                    t = nc.tensor.matmul(PH(h)[:, j, 0:2 * nh], m.ohT[:, h, j, :],
                                         m.node[:, bass.ds(blocks[j], 1), 0:2 * nh].rearrange("p o n -> p (o n)"),
                                         start=True, stop=True)
                t.then_inc(s.hs_ready, 1)
            if nh:
                scores(0, 0)

            def body(g, h, i, peeled):
                if nh:
                    scores(g + 1, 1 - h)
                else:
                    take(pe, s.oh_ready)
                if nh or weights is not None:
                    take(pe, s.msg_ready)
                else:
                    take(pe, s.landed)
                if not peeled:
                    take(pe, s.ps_free)
                for j in range(G):
                    t = nc.tensor.matmul(PM(h, j), m.oh[:, h, j, :], m.ring[:, h, j, 0:ncols],
                                         start=True, stop=not attr)
                    if attr:
                        t = nc.tensor.matmul(PM(h, j), m.oh[:, h, j, :], m.ring2[:, h, j, :], start=False, stop=True)
                t.then_inc(s.summed, 1)
            groups(pe, body)
            take(pe, s.ps_free, 2)
            if not nh:
                take(pe, s.oh_ready)

        @block.vector
        def _(v):
            V = nc.vector

            def seq(ins):
                ins.then_inc(s.ch, 1)
                take(v, s.ch)

            if ones:
                V.memset(m.ring[:, :, :, D:D + 1], 1.0)
            V.memset(m.rmax[:], -3e38)
            V.memset(m.A[:, :, col:col + ncols], 0.0).then_inc(s.ch, 1)
            take(v, s.ch)
            v.sem_inc(s.init)

            def one_hot(g, h):
                V.tensor_tensor(m.oh[:, h], bc(m.iota[:].unsqueeze(1), (P, G, P)),
                                bc(li[:, bass.ds(g * G, G)].unsqueeze(2), (P, G, P)), ALU.is_equal).then_inc(s.oh_ready, 1)

            def add_up(g, h):
                blocks = [v.value_load(bt[0:1, bass.ds(g * G + j, 1)], min_val=0, max_val=NB - 1) for j in range(G)]
                for j in range(G):
                    dst = m.A[:, bass.ds(blocks[j], 1), col:col + ncols].rearrange("p o n -> p (o n)")
                    V.tensor_tensor(dst, dst, PM(h, j), ALU.add).then_inc(s.added, 1)
                    take(v, s.added)
                v.sem_inc(s.ps_free)

            one_hot(0, 0)

            def body(g, h, i, peeled, first=False):
                if not first:
                    take(v, s.summed)
                    v.sem_inc(s.ring_free)
                one_hot(g + 1, 1 - h)
                sc, lr, dd = (x[:, h, :, 0:nh] for x in (m.sc, m.lr, m.dd)) if nh else (None,) * 3
                if nh:
                    take(v, s.landed)
                    take(v, s.hs_ready)
                    seq(V.tensor_tensor(sc, PH(h)[:, :, 0:nh], m.ring[:, h, :, D:D + nh], ALU.add))
                    seq(V.tensor_tensor(sc, sc, bc(m.neg[:, bass.ds(g * G, G)].unsqueeze(2), (P, G, nh)), ALU.add))
                    seq(V.scalar_tensor_tensor(out=lr, in0=sc, scalar=SLOPE, in1=sc, op0=ALU.mult, op1=ALU.max))
                    V.tensor_tensor(dd, lr, PH(h)[:, :, nh:2 * nh], ALU.subtract).then_inc(s.d_ready, 1)
                    if nh == 4:
                        seq(V.tensor_tensor(m.rmax[:], m.rmax[:], lr, ALU.max))
                if not first:
                    add_up(g - 1, 1 - h)
                if nh:
                    take(v, s.w_ready)
                    rows = m.ring[:, h, :, 0:D].rearrange("p j (n d) -> p j n d", n=nh)
                    w = bc(m.ring[:, h, :, D:D + nh].unsqueeze(3), (P, G, nh, D // nh))
                    V.tensor_tensor(rows, rows, w, ALU.mult).then_inc(s.msg_ready, 1)
                if weights is not None:
                    take(v, s.landed)
                    rows = m.ring[:, h, :, 0:width]
                    V.tensor_tensor(rows, rows, bc(weights[:, bass.ds(g * G, G)].unsqueeze(2), (P, G, width)),
                                    ALU.mult).then_inc(s.msg_ready, 1)
            body(0, 0, 0, True, first=True)
            body(1, 1, 0, True)
            with v.Fori(1, NG // 2) as i:
                for h in range(2):
                    body(2 * i + h, h, i, False)
            take(v, s.summed)
            add_up(NG - 1, 1)
            if nh:
                take(v, s.hs_ready)


def chunk(t, c, lo=0, hi=None):
    return t[:, bass.ds(c * CB, CB), lo:t.shape[2] if hi is None else hi]


def layer_norm(m, v, seq, dst, var_ready, std_ready):
    V = m.nc.vector
    mean, var, std, rstd = (m.st[:, k, :] for k in range(4))
    seq(V.tensor_reduce(mean, m.Y[:], AX, ALU.add))
    seq(V.tensor_scalar(mean, mean, -1.0 / D, None, ALU.mult))
    seq(V.tensor_tensor(m.Y[:], m.Y[:], bc(mean.unsqueeze(2), (P, CB, D)), ALU.add))
    seq(V.tensor_tensor(m.S[:], m.Y[:], m.Y[:], ALU.mult))
    seq(V.tensor_reduce(var, m.S[:], AX, ALU.add))
    V.tensor_scalar(var, var, 1.0 / D, EPS, ALU.mult, ALU.add).then_inc(var_ready, 1)
    take(v, std_ready)
    seq(V.reciprocal(rstd, std))
    return V.tensor_tensor(dst, m.Y[:], bc(rstd.unsqueeze(2), (P, CB, D)), ALU.mult)


def root(m, act, var_ready, std_ready):
    take(act, var_ready)
    m.nc.scalar.activation(m.st[:, 2, :], m.st[:, 1, :], ACT.Sqrt).then_inc(std_ready, 1)


def nodes_sage(m):
    nc = m.nc
    ch, mean_ok, tp, cp, mm, x_ok, vr, sr = (m.token(x) for x in (
        "ch", "mean", "transposed", "copied", "product", "x_ready", "var", "std"))
    o = m.sem("n0_stored")
    TP1 = m.PS[:, 0:2, :].rearrange("p k (j n) -> p (k j) n", j=4)
    TP2 = m.PS[:, 2:4, :].rearrange("p k (j n) -> p (k j) n", j=4)
    PO = m.PS[:, 4:6, :].rearrange("p k (j n) -> p (k j) n", j=4)
    with nc.Block() as block:
        @block.vector
        def _(v):
            V = nc.vector

            def seq(ins):
                ins.then_inc(ch, 1)
                take(v, ch)
            deg = m.rec[:, :, 0:1]
            seq(V.tensor_scalar(deg, m.A[:, :, D:D + 1], 1.0, None, ALU.max))
            seq(V.reciprocal(deg, deg))
            with v.Fori(0, NC) as c:
                V.tensor_copy(m.HR[:, :, 0:D], chunk(m.X, c)).then_inc(mean_ok, 1)
                V.tensor_tensor(m.M, chunk(m.A, c, 0, D), bc(chunk(m.rec, c, 0, 1), (P, CB, D)),
                                ALU.mult).then_inc(mean_ok, 1)
                take(v, mm)
                seq(V.tensor_tensor(m.Y[:], PO[:, 0:CB, :], chunk(m.X, c), ALU.add))
                layer_norm(m, v, seq, chunk(m.X, c), vr, sr).then_inc(x_ok, 1)

        @block.tensor
        def _(pe):
            with pe.Fori(0, NC) as c:
                take(pe, mean_ok, 2)
                for k in range(CB):
                    nc.tensor.transpose(TP1[:, k, :], m.HR[:, k, 0:D], m.ident[:])
                    t = nc.tensor.transpose(TP2[:, k, :], m.M[:, k, :], m.ident[:])
                t.then_inc(tp, 1)
                take(pe, cp, 2)
                for k in range(CB):
                    nc.tensor.matmul(PO[:, k, :], m.xT[:, k, :], m.w["self"][:], start=True, stop=False)
                    nc.tensor.matmul(PO[:, k, :], m.mT[:, k, :], m.w["neigh"][:], start=False, stop=False)
                    nc.tensor.matmul(PO[:, k, :], m.ones[0:1, :], m.bias[:, 0, :], start=False, stop=False)
                    t = nc.tensor.matmul(PO[:, k, :], m.ones[0:1, :], m.bias[:, 1, :], start=False, stop=True)
                t.then_inc(mm, 1)

        @block.scalar
        def _(act):
            with act.Fori(0, NC) as c:
                take(act, tp)
                nc.scalar.copy(m.xT, TP1[:, 0:CB, :]).then_inc(cp, 1)
                nc.scalar.copy(m.mT, TP2[:, 0:CB, :]).then_inc(cp, 1)
                root(m, act, vr, sr)

        @block.sync
        def _(sp):
            rows = m.tab1.rearrange("(b p) d -> p b d", p=P)
            with sp.Fori(0, NC) as c:
                take(sp, x_ok)
                sp.dma_start(rows[:, bass.ds(c * CB, CB), :], chunk(m.X, c)).then_inc(o, 16)
            sp.wait_ge(o, 16 * NC)


def nodes_project(m, tag, w, wa, nh, table, width, after_attention):
    nc = m.nc
    ch, x_ok, tp, cp, mm, h_ok, sc_ok, vr, sr, er, ed, mx, mxd, rows_free = (m.token(x) for x in (
        "ch", "x_ready", "transposed", "copied", "product", "h_ready", "sc_ready",
        "var", "std", "elu_in", "elu_out", "max_in", "max_out", "rows_free"))
    o = m.sem(tag + "_stored")
    TP1 = m.PS[:, 0:2, :].rearrange("p k (j n) -> p (k j) n", j=4)
    PO = m.PS[:, 4:6, :].rearrange("p k (j n) -> p (k j) n", j=4)
    PSC = m.PS[:, 6, 0:8 * CB].rearrange("p (j n) -> p j n", j=CB)
    with nc.Block() as block:
        @block.vector
        def _(v):
            V = nc.vector

            def seq(ins):
                ins.then_inc(ch, 1)
                take(v, ch)
            if after_attention:
                seq(V.tensor_reduce(m.gmax[:, 0:1], m.rmax[:].rearrange("p a b -> p (a b)"), AX, ALU.max))
                V.memset(m.tmp4[:], 0.0).then_inc(mx, 1)
                take(v, mxd)
                seq(V.tensor_scalar(m.tmp4[:], m.node[:, :, 4:8], m.gmax[:, 1:2], -1.0, ALU.subtract, ALU.mult))
                V.tensor_scalar(m.tmp4[:], m.tmp4[:], 0.0, None, ALU.add).then_inc(er, 1)
                take(v, ed)
                seq(V.scalar_tensor_tensor(out=m.rec[:], in0=m.tmp4[:], scalar=1e-8, in1=m.A[:, :, D:D + 4],
                                           op0=ALU.mult, op1=ALU.add))
                seq(V.reciprocal(m.rec[:], m.rec[:]))
            with v.Fori(0, NC) as c:
                x = chunk(m.X, c)
                if after_attention:
                    for j in range(4):
                        seq(V.tensor_tensor(m.M[:, :, 32 * j:32 * j + 32], chunk(m.A, c, 32 * j, 32 * j + 32),
                                            bc(chunk(m.rec, c, j, j + 1), (P, CB, 32)), ALU.mult))
                    V.tensor_scalar(m.S[:], m.M, 0.0, None, ALU.min).then_inc(er, 1)
                    take(v, ed)
                    seq(V.scalar_tensor_tensor(out=m.Y[:], in0=m.M, scalar=0.0, in1=m.S[:], op0=ALU.max, op1=ALU.add))
                    seq(V.scalar_tensor_tensor(out=m.Y[:], in0=m.Y[:], scalar=-1.0, in1=x, op0=ALU.add, op1=ALU.add))
                else:
                    seq(V.scalar_tensor_tensor(out=m.Y[:], in0=x, scalar=2.0, in1=chunk(m.A, c, 0, D),
                                               op0=ALU.mult, op1=ALU.add))
                layer_norm(m, v, seq, m.mT, vr, sr).then_inc(x_ok, 1)
                take(v, mm)
                seq(V.tensor_copy(chunk(m.nbr, c, 0, nh), PSC[:, :, 0:nh]))
                seq(V.tensor_copy(chunk(m.node, c, 0, nh), PSC[:, :, nh:2 * nh]))
                v.sem_inc(sc_ok)
            for j in range(nh):
                seq(V.tensor_reduce(m.gmax[:, j:j + 1], m.nbr[:, :, j], AX, ALU.max))
            v.sem_inc(mx)
            take(v, mxd)
            for j in range(nh):
                own, shift = m.node[:, :, j:j + 1], m.node[:, :, nh + j:nh + j + 1]
                seq(V.tensor_scalar(shift, own, m.sc[:, 0, 0, j:j + 1], None, ALU.add))
                seq(V.scalar_tensor_tensor(out=shift, in0=shift, scalar=SLOPE, in1=shift, op0=ALU.mult, op1=ALU.max))

        @block.gpsimd
        def _(pool):
            if after_attention:
                take(pool, mx)
                nc.gpsimd.partition_all_reduce(m.gmax[:, 1:2], m.gmax[:, 0:1], P, RMAX).then_inc(mxd, 1)
            take(pool, mx)
            nc.gpsimd.partition_all_reduce(m.sc[:, 0, 0, 0:nh], m.gmax[:, 0:nh], P, RMAX).then_inc(mxd, 1)

        @block.tensor
        def _(pe):
            with pe.Fori(0, NC) as c:
                take(pe, x_ok)
                for k in range(CB):
                    t = nc.tensor.transpose(TP1[:, k, :], m.mT[:, k, :], m.ident[:])
                t.then_inc(tp, 1)
                take(pe, cp, 2)
                for k in range(CB):
                    nc.tensor.matmul(PO[:, k, :], m.xT[:, k, :], w[:], start=True, stop=True)
                    t = nc.tensor.matmul(PSC[:, k, 0:2 * nh], m.xT[:, k, :], wa[:], start=True, stop=True)
                t.then_inc(h_ok, 1)

        @block.scalar
        def _(act):
            if after_attention:
                take(act, er)
                nc.scalar.activation(m.tmp4[:], m.tmp4[:], ACT.Exp).then_inc(ed, 1)

            with act.Fori(0, NC) as c:
                if after_attention:
                    take(act, er)
                    nc.scalar.activation(m.S[:], m.S[:], ACT.Exp).then_inc(ed, 1)
                root(m, act, vr, sr)
                take(act, tp)
                nc.scalar.copy(m.xT, TP1[:, 0:CB, :]).then_inc(cp, 1)
                nc.scalar.copy(chunk(m.X, c), m.mT).then_inc(cp, 1)
                take(act, h_ok)
                nc.scalar.copy(m.HR[:, :, 0:D], PO[:, 0:CB, :])
                nc.scalar.copy(m.HR[:, :, D:D + nh], PSC[:, :, 0:nh]).then_inc(mm, 1)
                take(act, rows_free)

        @block.sync
        def _(sp):
            rows = table.rearrange("(b p) d -> p b d", p=P)
            with sp.Fori(0, NC) as c:
                take(sp, sc_ok)
                sp.dma_start(rows[:, bass.ds(c * CB, CB), :], m.HR[:, :, 0:width]).then_inc(o, 16)
                sp.wait_ge(o, 16 * (c + 1))
                sp.sem_inc(rows_free)


def nodes_hop(m):
    nc = m.nc
    ch, ok, o = m.token("ch"), m.sem("n3_rows_ready"), m.sem("n3_stored")
    with nc.Block() as block:
        @block.vector
        def _(v):
            V = nc.vector

            def seq(ins):
                ins.then_inc(ch, 1)
                take(v, ch)
            den, r, t, u = m.A[:, :, D:D + 2], m.rec[:, :, 0:2], m.tmp4[:, :, 0:2], m.tmp4[:, :, 2:4]
            seq(V.tensor_scalar(t, den, 0.0, None, ALU.is_equal))
            seq(V.tensor_tensor(t, t, den, ALU.add))
            seq(V.reciprocal(r, t))
            seq(V.tensor_tensor(t, r, den, ALU.mult))
            seq(V.tensor_scalar(u, t, 0.0, None, ALU.is_equal))
            seq(V.tensor_tensor(u, u, t, ALU.add))
            seq(V.reciprocal(u, u))
            seq(V.tensor_tensor(r, r, u, ALU.mult))
            for i in (1, 0):
                rows = m.A[:, :, 64 * i:64 * i + 64]
                V.tensor_tensor(rows, rows, bc(m.rec[:, :, i:i + 1], (P, NB, 64)), ALU.mult).then_inc(ok, 1)

        @block.sync
        def _(sp):
            sp.wait_ge(ok, 1)
            sp.dma_start(m.tab4.rearrange("(b p) d -> p b d", p=P), m.A[:, :, 64:128]).then_inc(o, 16)
            sp.wait_ge(o, 16)


def nodes_final(m):
    nc = m.nc
    ch, gi_, go, ok, vr, sr = (m.token(x) for x in ("ch", "elu_in", "elu_out", "x_ready", "var", "std"))
    o = m.sem("n4_stored")
    with nc.Block() as block:
        @block.vector
        def _(v):
            V = nc.vector

            def seq(ins):
                ins.then_inc(ch, 1)
                take(v, ch)
            full = (P, CB, D)
            with v.Fori(0, NC) as c:
                seq(V.tensor_scalar(m.Y[:, :, 0:64], chunk(m.A, c, 0, 64), 0.0, None, ALU.add))
                seq(V.tensor_tensor(m.Y[:, :, 64:128], chunk(m.A, c, 64, 128), bc(chunk(m.rec, c, 1, 2), (P, CB, 64)), ALU.mult))
                seq(V.tensor_tensor(m.xT.bitcast(I32), m.Y[:], m.Y[:], ALU.is_equal))
                seq(V.memset(m.M, 0.0))
                seq(V.copy_predicated(m.M, m.xT.bitcast(I32), m.Y[:]))
                seq(V.tensor_tensor(m.M, m.M, bc(m.w["b3"][:].unsqueeze(1), full), ALU.add))
                seq(V.tensor_tensor(m.S[:], m.M, bc(m.w["fc3"][:].unsqueeze(1), full), ALU.mult))
                seq(V.tensor_reduce(m.gg[:], m.S[:].rearrange("p b (i d) -> p b i d", i=2), AX, ALU.add))
                V.tensor_tensor(m.gg[:], m.gg[:], bc(m.bf3[:].unsqueeze(1), (P, CB, 2)), ALU.add).then_inc(gi_, 1)
                take(v, go)
                seq(V.tensor_scalar(m.gg[:], m.gg[:], 1.0, None, ALU.add))
                seq(V.reciprocal(m.gg[:], m.gg[:]))
                seq(V.tensor_scalar(m.S[:], m.M, 0.0, None, ALU.min))
                for i in range(2):
                    h = m.S[:, :, 64 * i:64 * i + 64]
                    seq(V.tensor_tensor(h, h, bc(m.gg[:, :, i:i + 1], (P, CB, 64)), ALU.mult))
                seq(V.scalar_tensor_tensor(out=m.M, in0=m.M, scalar=0.0, in1=m.S[:], op0=ALU.max, op1=ALU.add))
                seq(V.scalar_tensor_tensor(out=m.M, in0=m.M, scalar=SLOPE, in1=m.M, op0=ALU.mult, op1=ALU.max))
                seq(V.tensor_tensor(m.Y[:], m.M, chunk(m.X, c), ALU.add))
                seq(layer_norm(m, v, seq, chunk(m.X, c), vr, sr))
                v.sem_inc(ok)

        @block.scalar
        def _(act):
            with act.Fori(0, NC) as c:
                take(act, gi_)
                nc.scalar.activation(m.gg[:], m.gg[:], ACT.Exp, scale=-1.0).then_inc(go, 1)
                root(m, act, vr, sr)

        @block.sync
        def _(sp):
            full = (NB - 1) * P
            rows = m.out[0:full, :].rearrange("(b p) d -> p b d", p=P)
            with sp.Fori(0, NC - 1) as c:
                take(sp, ok)
                sp.dma_start(rows[:, bass.ds(c * CB, CB), :], chunk(m.X, c)).then_inc(o, 16)
            take(sp, ok)
            b = (NC - 1) * CB
            sp.dma_start(rows[:, b:NB - 1, :], m.X[:, b:NB - 1, :]).then_inc(o, 16)
            sp.dma_start(m.out[full:N, :], m.X[0:LAST, NB - 1, :]).then_inc(o, 16)
            sp.wait_ge(o, 16 * (NC + 1))


NAMES = ["x", "src", "dst", "edge_attr_128", "L0_gnn_W_self", "L0_gnn_b_self", "L0_gnn_W_neigh", "L0_gnn_b_neigh",
         "L2_gnn_W", "L2_gnn_A_left", "L2_gnn_A_right", "L3_gnn_W", "L3_gnn_b", "L3_gnn_fc", "L3_gnn_bf",
         "L3_gnn_a_src", "L3_gnn_a_dst"]


def kernel(**inputs):
    import numpy as np
    import concourse.bacc as bacc
    from concourse.bass_utils import run_bass_kernel_spmd

    nc = bacc.Bacc("TRN2", target_bir_lowering=False, num_devices=1)
    arrays, aps = {}, {}
    for name in NAMES:
        arr = np.ascontiguousarray(inputs[name])
        arrays["in_" + name] = arr
        aps[name] = nc.dram_tensor("in_" + name, arr.shape, mybir.dt.from_np(arr.dtype), kind="ExternalInput").ap()
    out = nc.dram_tensor("out_0", (N, D), F32, kind="ExternalOutput").ap()
    build(nc, aps, out)
    r = run_bass_kernel_spmd(nc, [arrays], core_ids=[0])
    return r.results[0]["out_0"]
```

```python
from contextlib import ExitStack

import concourse.bass as bass
from concourse import mybir
from concourse.alu_op_type import AluOpType as ALU

ACT = mybir.ActivationFunctionType
F32 = mybir.dt.float32
I32 = mybir.dt.int32
AX = mybir.AxisListType.X
RMAX = bass.bass_isa.ReduceOp.max

P = 128
D = 128
N = 12500
E = 200000
NB = -(-N // P)
LAST = N - (NB - 1) * P
EP = 125
EC = E // EP
G = 4
R = 4
T = -(-((E + NB * (P - 1)) // P) // (R * G)) * (R * G)
NG = T // G
CB = 7
NC = NB // CB
RW = 132
NO_NODE = 255
EPS = 1e-5
SLOPE = 0.2


class Parts:
    pass


def take(eng, sem, n=1):
    eng.wait_ge(sem, n).then_inc(sem, -n)


def bc(ap, shape):
    return ap.broadcast_to(list(shape))


def build(nc, a, out):
    with ExitStack() as ctx:
        def sb(name, shape, dt=F32):
            return ctx.enter_context(nc.sbuf_tensor(name, shape, dt))

        m = Parts()
        m.nc, m.a, m.out = nc, a, out
        m.sem = lambda name: ctx.enter_context(nc.semaphore(name))
        tokens = {}

        def token(name):
            if name not in tokens:
                tokens[name] = m.sem(name)
            return tokens[name]
        m.token = token

        def dram(name, shape, dt=F32):
            return nc.dram_tensor(name, shape, dt).ap()
        m.rec_dst = dram("rec_by_dst", (P * T, 4), I32)
        m.rec_src = dram("rec_by_src", (P * T, 4), I32)
        m.tab1 = dram("x1_rows", (NB * P, D))
        m.tab2 = dram("h2_rows", (NB * P, RW))
        m.tab3 = dram("h3_rows", (NB * P, D + 2))
        m.tab4 = dram("hop_rows", (NB * P, 64))

        m.X = sb("X", [P, NB, D])
        m.A = sb("A", [P, NB, RW])
        m.gi_d, m.gi_s = sb("gi_d", [P, T], I32), sb("gi_s", [P, T], I32)
        m.ei_d = sb("ei_d", [P, T], I32)
        m.li_d, m.li_s = sb("li_d", [P, T]), sb("li_s", [P, T])
        m.neg = sb("neg", [P, T])
        m.w1 = m.ei_d[:].bitcast(F32)
        m.bt_d, m.bt_s = sb("bt_d", [1, NG], I32), sb("bt_s", [1, NG], I32)
        m.ring = sb("ring", [P, R, G, RW])
        m.ring2 = sb("ring2", [P, R, G, D])
        m.idx = sb("idx", [P, R, 2 * G], I32)
        m.oh = sb("oh", [P, R, G, P])
        m.ohT = sb("ohT", [P, 2, G, P])
        m.sc = sb("sc", [P, 2, G, 4])
        m.lr = sb("lr", [P, 2, G, 4])
        m.dd = sb("dd", [P, 2, G, 4])
        m.rmax = sb("rmax", [P, G, 4])
        m.gmax = sb("gmax", [P, 4])
        m.node = sb("node", [P, NB, 8])
        m.nbr = sb("nbr", [P, NB, 4])
        m.rec = sb("rec", [P, NB, 4])
        m.tmp4 = sb("tmp4", [P, NB, 4])
        m.iota = sb("iota", [P, P])
        m.pidx = sb("pidx", [P, 1])
        m.ident = sb("ident", [P, P])
        m.tri = sb("tri", [P, P])
        m.ones = sb("ones", [P, P])
        m.iota_b = sb("iota_b", [P, NB])
        m.w = {n: sb("w_" + n, [P, D]) for n in ("self", "neigh", "l2", "l3", "t1", "b3", "fc3")}
        m.wa2, m.wa3 = sb("wa2", [P, 8]), sb("wa3", [P, 4])
        m.bd = sb("bd", [P, 12])
        m.bias = sb("bias", [1, 2, D])
        m.bf3 = sb("bf3", [P, 2])
        m.Y = sb("Y", [P, CB, D])
        m.S = sb("S", [P, CB, D])
        ring_view = lambda t: t[:].rearrange("p h j n -> p (h j) n")[:, 0:CB, :]
        m.M, m.xT, m.mT = ring_view(m.oh), ring_view(m.ohT), ring_view(m.ring2)
        m.HR = sb("HR", [P, CB, RW])
        m.st = sb("st", [P, 4, CB])
        m.gg = sb("gg", [P, CB, 2])
        m.PS = ctx.enter_context(nc.psum_tensor("PS", [P, 8, 512], F32))

        prepare(m)
        group_edges(m, "d", a["dst"], a["src"], m.rec_dst, m.gi_d, m.li_d, m.ei_d, m.bt_d)
        group_edges(m, "s", a["src"], a["dst"], m.rec_src, m.gi_s, m.li_s, None, m.bt_s)
        load_nodes(m)
        edge_pass(m, "e0", a["x"], D, m.gi_d, m.li_d, m.bt_d, 0, D + 1, ones=True)
        nodes_sage(m)
        edge_pass(m, "e1", m.tab1, D, m.gi_d, m.li_d, m.bt_d, 0, D, attr=True)
        nodes_project(m, "n1", m.w["l2"], m.wa2, 4, m.tab2, D + 4, after_attention=False)
        edge_pass(m, "e2", m.tab2, D + 4, m.gi_s, m.li_s, m.bt_s, 0, D + 4, heads=4)
        nodes_project(m, "n2", m.w["l3"], m.wa3, 2, m.tab3, D + 2, after_attention=True)
        edge_pass(m, "e3", m.tab3, D + 2, m.gi_s, m.li_s, m.bt_s, 0, D + 2, heads=2)
        nodes_hop(m)
        edge_pass(m, "e4", m.tab4, 64, m.gi_s, m.li_s, m.bt_s, 64, 64, weights=m.w1)
        nodes_final(m)


def prepare(m):
    nc, a = m.nc, m.a
    loaded, made, step = m.sem("w_loaded"), m.sem("const_made"), m.sem("w_step")
    pe_done, copied, zeroed = m.sem("w_pe"), m.sem("w_copied"), m.sem("w_zeroed")
    n_loads = 10 + 8 + 4
    with nc.Block() as block:
        @block.sync
        def _(sp):
            sp.dma_start(m.w["self"][:], a["L0_gnn_W_self"]).then_inc(loaded, 16)
            sp.dma_start(m.w["neigh"][:], a["L0_gnn_W_neigh"]).then_inc(loaded, 16)
            sp.dma_start(m.w["l2"][:], a["L2_gnn_W"]).then_inc(loaded, 16)
            for i in range(2):
                sp.dma_start(m.w["l3"][:, 64 * i:64 * i + 64], a["L3_gnn_W"][i]).then_inc(loaded, 16)
            sp.dma_start(m.bias[:, 0, :], a["L0_gnn_b_self"].rearrange("(o d) -> o d", o=1)).then_inc(loaded, 16)
            sp.dma_start(m.bias[:, 1, :], a["L0_gnn_b_neigh"].rearrange("(o d) -> o d", o=1)).then_inc(loaded, 16)
            sp.dma_start(m.w["b3"][:], a["L3_gnn_b"].rearrange("i d -> (i d)").partition_broadcast(P)).then_inc(loaded, 16)
            sp.dma_start(m.w["fc3"][:], a["L3_gnn_fc"].rearrange("i d o -> (i d o)").partition_broadcast(P)).then_inc(loaded, 16)
            sp.dma_start(m.bf3[:], a["L3_gnn_bf"].partition_broadcast(P)).then_inc(loaded, 16)
            sp.wait_ge(zeroed, 1)
            for h in range(4):
                sp.dma_start(m.bd[32 * h:32 * h + 32, h:h + 1], a["L2_gnn_A_right"][h]).then_inc(loaded, 16)
                sp.dma_start(m.bd[32 * h:32 * h + 32, 4 + h:5 + h], a["L2_gnn_A_left"][h]).then_inc(loaded, 16)
            for i in range(2):
                for col, name in ((8, "L3_gnn_a_dst"), (10, "L3_gnn_a_src")):
                    sp.dma_start(m.bd[64 * i:64 * i + 64, col + i:col + i + 1],
                                 a[name][i].rearrange("(d o) -> d o", o=1)).then_inc(loaded, 16)

        @block.gpsimd
        def _(pool):
            kw = dict(allow_small_or_imprecise_dtypes=True)
            nc.gpsimd.iota(m.iota[:], [[1, P]], base=0, channel_multiplier=0, **kw).then_inc(made, 1)
            nc.gpsimd.iota(m.pidx[:], [[0, 1]], base=0, channel_multiplier=1, **kw).then_inc(made, 1)
            nc.gpsimd.iota(m.iota_b[:], [[1, NB]], base=0, channel_multiplier=0, **kw).then_inc(made, 1)
            nc.gpsimd.memset(m.ones[:], 1.0).then_inc(made, 1)

        @block.vector
        def _(v):
            nc.vector.memset(m.bd[:], 0.0).then_inc(zeroed, 1)
            v.wait_ge(made, 4)
            nc.vector.tensor_scalar(m.ident[:], m.iota[:], m.pidx[:], None, ALU.is_equal).then_inc(step, 1)
            nc.vector.tensor_scalar(m.tri[:], m.iota[:], m.pidx[:], None, ALU.is_gt).then_inc(step, 1)
            v.wait_ge(loaded, 16 * n_loads)
            v.wait_ge(pe_done, 1)
            nc.vector.tensor_copy(m.w["self"][:], m.PS[:, 0, 0:D]).then_inc(copied, 1)
            nc.vector.tensor_copy(m.w["neigh"][:], m.PS[:, 1, 0:D]).then_inc(copied, 1)
            nc.vector.tensor_copy(m.w["t1"][:], m.PS[:, 2, 0:D]).then_inc(copied, 1)
            nc.vector.tensor_copy(m.M[:, 0, :], m.PS[:, 3, 0:D]).then_inc(copied, 1)
            v.wait_ge(pe_done, 2)
            nc.vector.tensor_copy(m.wa2[:], m.PS[:, 4, 0:8]).then_inc(copied, 1)
            nc.vector.tensor_copy(m.wa3[:], m.PS[:, 5, 0:4]).then_inc(copied, 1)

        @block.tensor
        def _(pe):
            pe.wait_ge(loaded, 16 * n_loads)
            pe.wait_ge(step, 2)
            for k, name in enumerate(("self", "neigh", "l2", "l3")):
                t = nc.tensor.transpose(m.PS[:, k, 0:D], m.w[name][:], m.ident[:])
            t.then_inc(pe_done, 1)
            pe.wait_ge(copied, 4)
            nc.tensor.matmul(m.PS[:, 4, 0:8], m.w["t1"][:], m.bd[:, 0:8], start=True, stop=True)
            nc.tensor.matmul(m.PS[:, 5, 0:4], m.M[:, 0, :], m.bd[:, 8:12], start=True, stop=True).then_inc(pe_done, 1)


def group_edges(m, tag, key, other, rec, gi, li, ei, bt):
    nc = m.nc
    A = m.A[:].rearrange("p b w -> p (b w)")
    Xf = m.X[:].rearrange("p b w -> p (b w)")
    AI, XI = A.bitcast(I32), Xf.bitcast(I32)
    recs = AI[0:EP, 0:4 * EC].rearrange("p (c w) -> p c w", w=4)
    k_i = AI[0:EP, 4 * EC:5 * EC]
    blk = A[0:EP, 5 * EC:6 * EC]
    mask = AI[0:EP, 6 * EC:7 * EC]
    run = A[0:EP, 7 * EC:8 * EC]
    pos = Xf[0:EP, 0:EC]
    row = XI[0:EP, EC:2 * EC]
    oth = XI[0:EP, 2 * EC:3 * EC]
    hi = XI[0:EP, 3 * EC:4 * EC]
    zero = Xf[0:EP, 4 * EC:5 * EC]
    fill = XI[:, 5 * EC:5 * EC + 2 * G * 4].rearrange("p (t w) -> p t w", w=4)
    small = Xf[:, 5 * EC + 64:5 * EC + 64 + 6 * NB].rearrange("p (k b) -> p k b", b=NB)
    smalli = XI[:, 5 * EC + 64 + 6 * NB:5 * EC + 64 + 7 * NB]
    icol = Xf[0:NB, 5 * EC + 64 + 7 * NB:5 * EC + 65 + 7 * NB]
    cnt, tiles, incl, base = (small[:, k, :] for k in range(4))
    iota_t = Xf[0:NB, 9000:9000 + T]
    cmp = Xf[0:NB, 10680:10680 + T]
    of_tile = m.neg[0:1, 0:T].bitcast(I32)
    back = AI[:, 0:4 * T].rearrange("p (t w) -> p t w", w=4)
    slots = m.idx[0:EP]
    rring = m.ring2[:].bitcast(I32)

    loaded, filled, fill_out = (m.sem(tag + x) for x in ("_loaded", "_fill", "_fill_out"))
    ch, cnt_ok, psum_ok, col_ok, cmp_ok, bt_ok, pos_ok = (
        m.sem(tag + x) for x in ("_ch", "_cnt", "_psum", "_col", "_cmp", "_bt", "_pos"))
    ring_ok, scattered, seen, back_ok, io = (m.sem(tag + "_ring"), [m.sem(f"{tag}_sc{h}") for h in range(2)],
                                             m.sem(tag + "_seen"), m.sem(tag + "_back"), m.sem(tag + "_iota"))
    NGE = EC // G
    with nc.Block() as block:
        @block.sync
        def _(sp):
            sp.dma_start(k_i, key.rearrange("(p c) -> p c", c=EC)).then_inc(loaded, 16)
            sp.dma_start(oth, other.rearrange("(p c) -> p c", c=EC)).then_inc(loaded, 16)
            sp.wait_ge(filled, 1)
            r = rec.rearrange("(p t) w -> p t w", p=P)
            for c in range(T // (2 * G)):
                sp.dma_start(r[:, 2 * G * c:2 * G * (c + 1), :], fill).then_inc(fill_out, 16)
            for h in range(2):
                sp.wait_ge(scattered[h], 16 * G)
                sp.sem_inc(seen)
            with sp.Fori(1, NGE // 2) as i:
                for h in range(2):
                    sp.wait_ge(scattered[h], 16 * G * (i + 1))
                    sp.sem_inc(seen)
            sp.dma_start(back, rec.rearrange("(p t) w -> p t w", p=P)).then_inc(back_ok, 16)

        @block.gpsimd
        def _(pool):
            nc.gpsimd.iota(iota_t, [[1, T]], base=0, channel_multiplier=0,
                           allow_small_or_imprecise_dtypes=True).then_inc(io, 1)
            pool.wait_ge(fill_out, 16 * (T // (2 * G)))
            with pool.Fori(0, NGE // 2) as i:
                for h in range(2):
                    take(pool, ring_ok)
                    for j in range(G):
                        nc.gpsimd.indirect_dma_start(
                            out=rec, out_offset=bass.IndirectOffsetOnAxis(ap=slots[:, h, j:j + 1], axis=0),
                            in_=rring[0:EP, h, j, 0:4], in_offset=None).then_inc(scattered[h], 16)

        @block.scalar
        def _(act):
            act.wait_ge(pos_ok, 1)

            def fill_ring(g, h):
                nc.scalar.copy(slots[:, h, 0:G], row[:, bass.ds(g * G, G)])
                nc.scalar.copy(rring[0:EP, h, :, 0:4], recs[:, bass.ds(g * G, G), :]).then_inc(ring_ok, 1)
            fill_ring(0, 0)
            fill_ring(1, 1)
            with act.Fori(1, NGE // 2) as i:
                for h in range(2):
                    take(act, seen)
                    fill_ring(2 * i + h, h)

        @block.tensor
        def _(pe):
            pe.wait_ge(cnt_ok, 1)
            nc.tensor.matmul(m.PS[:, 0, 0:NB], m.ones[0:EP, :], cnt[0:EP, :], start=True, stop=True)
            nc.tensor.matmul(m.PS[:, 1, 0:NB], m.tri[0:EP, :], cnt[0:EP, :], start=True, stop=True).then_inc(psum_ok, 1)
            pe.wait_ge(col_ok, 1)
            nc.tensor.transpose(m.PS[0:NB, 2, 0:P], incl, m.ident[:]).then_inc(psum_ok, 1)
            pe.wait_ge(cmp_ok, 1)
            q = T // 4
            for k in range(4):
                t = nc.tensor.matmul(m.PS[0:1, 3 + k, 0:q], m.ones[0:NB, 0:1], cmp[:, q * k:q * k + q],
                                     start=True, stop=True)
            t.then_inc(bt_ok, 1)

        @block.vector
        def _(v):
            def seq(ins):
                ins.then_inc(ch, 1)
                take(v, ch)
            V = nc.vector
            V.memset(fill, 0)
            seq(V.memset(zero, 0.0))
            V.memset(fill[:, :, 1:2], NO_NODE).then_inc(filled, 1)
            seq(V.memset(cnt, 0.0))
            seq(V.memset(pos, 0.0))
            v.wait_ge(loaded, 32)
            seq(V.tensor_scalar(hi, k_i, 7, None, ALU.logical_shift_right))
            seq(V.tensor_copy(blk, hi))
            seq(V.tensor_copy(recs[:, :, 0], oth))
            seq(V.tensor_scalar(recs[:, :, 1], k_i, P - 1, None, ALU.bitwise_and))
            seq(V.tensor_scalar(run, zero, 1.0, None, ALU.add))
            seq(V.tensor_tensor_scan(pos, run, zero, -1.0, ALU.add, ALU.add))
            seq(V.tensor_scalar(small[0:EP, 5, 0:1], m.pidx[0:EP, :], float(EC), None, ALU.mult))
            seq(V.tensor_scalar(recs[:, :, 2], pos, small[0:EP, 5, 0:1], None, ALU.add))
            seq(V.tensor_copy(recs[:, :, 3], zero))
            with v.Fori(0, NB) as b:
                seq(V.tensor_scalar(run, blk, m.iota_b[0:EP, bass.ds(b, 1)], None, ALU.is_equal, ALU.add,
                                    accum_out=cnt[0:EP, bass.ds(b, 1)]))
            V.memset(small[:, 4, :], 0.0).then_inc(cnt_ok, 1)
            v.wait_ge(psum_ok, 1)
            seq(V.tensor_scalar(tiles, m.PS[:, 0, 0:NB], float(P - 1), None, ALU.add))
            seq(V.tensor_copy(smalli, tiles))
            seq(V.tensor_scalar(smalli, smalli, 7, None, ALU.logical_shift_right))
            seq(V.tensor_copy(tiles, smalli))
            seq(V.tensor_tensor_scan(incl, tiles, small[:, 4, :], 0.0, ALU.add, ALU.add))
            seq(V.tensor_tensor(base, incl, tiles, ALU.subtract))
            seq(V.tensor_scalar(base, base, float(P), -1.0, ALU.mult, ALU.add))
            seq(V.tensor_tensor(base, base, m.PS[:, 1, 0:NB], ALU.add))
            V.memset(small[:, 5, :], 0.0).then_inc(col_ok, 1)
            v.wait_ge(psum_ok, 2)
            v.wait_ge(io, 1)
            seq(V.tensor_copy(icol, m.PS[0:NB, 2, 0:1]))
            V.tensor_scalar(cmp, iota_t, icol, None, ALU.is_ge).then_inc(cmp_ok, 1)
            v.wait_ge(bt_ok, 1)
            q = T // 4
            for k in range(4):
                seq(V.tensor_scalar(of_tile[:, q * k:q * k + q], m.PS[0:1, 3 + k, 0:q], float(NB - 1), None, ALU.min))
            four = of_tile.rearrange("o (g j) -> o g j", j=G)
            for j in range(G):
                if j:
                    seq(V.tensor_scalar(four[:, :, j], four[:, :, j], 7 * j, None, ALU.logical_shift_left))
                    seq(V.tensor_tensor(bt[:], bt[:], four[:, :, j], ALU.bitwise_or))
                else:
                    seq(V.tensor_copy(bt[:], four[:, :, 0]))
            with v.Fori(0, NB) as b:
                seq(V.tensor_scalar(mask, blk, m.iota_b[0:EP, bass.ds(b, 1)], None, ALU.is_equal))
                seq(V.tensor_copy(small[0:EP, 5, 0:1], base[0:EP, bass.ds(b, 1)]))
                seq(V.tensor_tensor_scan(run, mask, zero, small[0:EP, 5, 0:1], ALU.add, ALU.add))
                seq(V.copy_predicated(pos, mask, run))
            seq(V.tensor_copy(row, pos))
            seq(V.tensor_scalar(hi, row, 7, None, ALU.logical_shift_right))
            seq(V.tensor_scalar(row, row, P - 1, None, ALU.bitwise_and))
            V.scalar_tensor_tensor(out=row, in0=row, scalar=float(T), in1=hi, op0=ALU.mult, op1=ALU.add).then_inc(pos_ok, 1)
            v.wait_ge(back_ok, 16)
            V.tensor_copy(gi[:, 0:T], back[:, :, 0])
            seq(V.tensor_copy(li[:, 0:T], back[:, :, 1]))
            if ei is not None:
                V.tensor_copy(ei[:, 0:T], back[:, :, 2])
            else:
                V.tensor_scalar(m.neg[:], li[:], float(NO_NODE), -1e30, ALU.is_equal, ALU.mult)


def load_nodes(m):
    nc = m.nc
    z, ld = m.sem("x_zero"), m.sem("x_loaded")
    with nc.Block() as block:
        @block.vector
        def _(v):
            nc.vector.memset(m.X[:, NB - 1, :], 0.0).then_inc(z, 1)

        @block.sync
        def _(sp):
            full = (NB - 1) * P
            sp.dma_start(m.X[:, 0:NB - 1, :], m.a["x"][0:full, :].rearrange("(b p) d -> p b d", p=P)).then_inc(ld, 16)
            sp.wait_ge(z, 1)
            sp.dma_start(m.X[0:LAST, NB - 1, :], m.a["x"][full:N, :]).then_inc(ld, 16)
            sp.wait_ge(ld, 32)


def tile_blocks(m, eng, bt, g):
    word = eng.value_load(bt[0:1, bass.ds(g, 1)], min_val=0, max_val=(1 << (7 * G)) - 1)
    return [m.nc.s_assert_within((word >> (7 * j)) & 127, 0, NB - 1,
                                 skip_runtime_bounds_check_because="the packed blocks are at most NB - 1")
            for j in range(G)]


def edge_pass(m, tag, table, width, gi, li, bt, col, ncols, ones=False, attr=False, heads=0, weights=None):
    nc = m.nc
    per = 2 * G if attr else G
    got = [m.sem(f"{tag}_got{h}") for h in range(R)]
    s = Parts()
    s.idx_ready = m.token("idx_ready")
    s.idx_free = m.token("idx_free")
    s.ring_free = m.token("ring_free")
    s.landed = m.token("landed")
    s.oh_ready = m.token("oh_ready")
    s.summed = m.token("summed")
    s.ps_free = m.token("ps_free")
    s.added = m.token("added")
    s.ohT_psum = m.token("ohT_psum")
    s.ohT_ready = m.token("ohT_ready")
    s.hs_ready = m.token("hs_ready")
    s.d_ready = m.token("d_ready")
    s.w_ready = m.token("w_ready")
    s.msg_ready = m.token("msg_ready")
    s.ch = m.token("ch")
    s.init = m.token("init")
    PM = lambda g, j: m.PS[:, 2 * (g % 2) + j // 2, RW * (j % 2):RW * (j % 2) + ncols]
    PT = lambda g: m.PS[:, 4 + g % 2, :].rearrange("p (j n) -> p j n", j=G)
    PH = lambda g: m.PS[:, 6 + g % 2, 0:8 * G].rearrange("p (j n) -> p j n", j=G)
    nh = heads

    def groups(eng, body):
        for h in range(R):
            body(h, h, 0)
        with eng.Fori(1, NG // R - 1) as i:
            for h in range(R):
                body(R * i + h, h, i)
        for h in range(R):
            body(NG - R + h, h, NG // R - 1)

    def exists(g):
        return not isinstance(g, int) or 0 <= g < NG

    with nc.Block() as block:
        @block.sync
        def _(sp):
            def body(g, h, i):
                sp.wait_ge(got[h], 16 * per * (i + 1))
                sp.sem_inc(s.idx_free)
                sp.sem_inc(s.landed)
            groups(sp, body)

        @block.gpsimd
        def _(pool):
            def body(g, h, i):
                take(pool, s.idx_ready)
                if exists(g - R):
                    take(pool, s.ring_free)
                for j in range(G):
                    nc.gpsimd.indirect_dma_start(
                        out=m.ring[:, h, j, 0:width], out_offset=None, in_=table,
                        in_offset=bass.IndirectOffsetOnAxis(ap=m.idx[:, h, j:j + 1], axis=0)).then_inc(got[h], 16)
                    if attr:
                        nc.gpsimd.indirect_dma_start(
                            out=m.ring2[:, h, j, :], out_offset=None, in_=m.a["edge_attr_128"],
                            in_offset=bass.IndirectOffsetOnAxis(ap=m.idx[:, h, G + j:G + j + 1], axis=0)
                        ).then_inc(got[h], 16)
            groups(pool, body)
            take(pool, s.ring_free, R)

        @block.scalar
        def _(act):
            def indices(g, h):
                ins = nc.scalar.copy(m.idx[:, h, 0:G], gi[:, bass.ds(g * G, G)])
                if attr:
                    ins = nc.scalar.copy(m.idx[:, h, G:2 * G], m.ei_d[:, bass.ds(g * G, G)])
                ins.then_inc(s.idx_ready, 1)

            def transposed(h):
                take(act, s.ohT_psum)
                nc.scalar.copy(m.ohT[:, h % 2], PT(h)).then_inc(s.ohT_ready, 1)

            def weigh(g, h):
                take(act, s.d_ready)
                nc.scalar.activation(m.ring[:, h % R, :, D:D + nh], m.dd[:, h % 2, :, 0:nh], ACT.Exp).then_inc(s.w_ready, 1)
                if nh == 2:
                    nc.scalar.activation(m.w1[:, bass.ds(g * G, G)], m.dd[:, h % 2, :, 1], ACT.Exp)

            for g in range(R):
                indices(g, g)
            if nh:
                transposed(0)
                transposed(1)
                weigh(0, 0)

            def body(g, h, i):
                if nh and exists(g + 2):
                    transposed(h + 2)
                if nh and exists(g + 1):
                    weigh(g + 1, h + 1)
                take(act, s.idx_free)
                if exists(g + R):
                    indices(g + R, h)
            groups(act, body)

        @block.tensor
        def _(pe):
            take(pe, s.init)

            def turn(h):
                take(pe, s.oh_ready)
                for j in range(G):
                    t = nc.tensor.transpose(PT(h)[:, j, :], m.oh[:, h % R, j, :], m.ident[:])
                t.then_inc(s.ohT_psum, 1)

            def scores(g, h):
                blocks = tile_blocks(m, pe, bt, g)
                take(pe, s.ohT_ready)
                for j in range(G):
                    t = nc.tensor.matmul(PH(h)[:, j, 0:2 * nh], m.ohT[:, h % 2, j, :],
                                         m.node[:, bass.ds(blocks[j], 1), 0:2 * nh].rearrange("p o n -> p (o n)"),
                                         start=True, stop=True)
                t.then_inc(s.hs_ready, 1)
            if nh:
                for g in (0, 1):
                    turn(g)
                    scores(g, g)

            def body(g, h, i):
                if nh and exists(g + 2):
                    turn(h + 2)
                if not nh:
                    take(pe, s.oh_ready)
                if nh or weights is not None:
                    take(pe, s.msg_ready)
                else:
                    take(pe, s.landed)
                if exists(g - 2):
                    take(pe, s.ps_free)
                for j in range(G):
                    t = nc.tensor.matmul(PM(h, j), m.oh[:, h, j, :], m.ring[:, h, j, 0:ncols],
                                         start=True, stop=not attr)
                    if attr:
                        t = nc.tensor.matmul(PM(h, j), m.oh[:, h, j, :], m.ring2[:, h, j, :], start=False, stop=True)
                t.then_inc(s.summed, 1)
                if nh and exists(g + 2):
                    scores(g + 2, h + 2)
            groups(pe, body)
            take(pe, s.ps_free, 2)

        @block.vector
        def _(v):
            V = nc.vector
            if ones:
                V.memset(m.ring[:, :, :, D:D + 1], 1.0)
            V.memset(m.rmax[:], -3e38)
            V.memset(m.A[:, :, col:col + ncols], 0.0).then_inc(s.ch, 1)
            take(v, s.ch)
            v.sem_inc(s.init)

            def one_hot(g, h):
                V.tensor_tensor(m.oh[:, h % R], bc(m.iota[:].unsqueeze(1), (P, G, P)),
                                bc(li[:, bass.ds(g * G, G)].unsqueeze(2), (P, G, P)), ALU.is_equal).then_inc(s.oh_ready, 1)

            def add_up(g, h):
                blocks = tile_blocks(m, v, bt, g)
                take(v, s.summed)
                v.sem_inc(s.ring_free)
                for j in range(G):
                    dst = m.A[:, bass.ds(blocks[j], 1), col:col + ncols].rearrange("p o n -> p (o n)")
                    if j:
                        v.wait_ge(s.added, j)
                    V.tensor_tensor(dst, dst, PM(h, j), ALU.add).then_inc(s.added, 1)
                take(v, s.added, G)
                v.sem_inc(s.ps_free)

            def exponents(g, h):
                sc, lr, dd = (x[:, h % 2, :, 0:nh] for x in (m.sc, m.lr, m.dd))
                take(v, s.landed)
                take(v, s.hs_ready)
                V.tensor_tensor(sc, PH(h)[:, :, 0:nh], m.ring[:, h % R, :, D:D + nh], ALU.add).then_inc(s.ch, 1)
                v.wait_ge(s.ch, 1)
                V.tensor_tensor(sc, sc, bc(m.neg[:, bass.ds(g * G, G)].unsqueeze(2), (P, G, nh)), ALU.add).then_inc(s.ch, 1)
                v.wait_ge(s.ch, 2)
                V.scalar_tensor_tensor(out=lr, in0=sc, scalar=SLOPE, in1=sc, op0=ALU.mult, op1=ALU.max).then_inc(s.ch, 1)
                v.wait_ge(s.ch, 3)
                V.tensor_tensor(dd, lr, PH(h)[:, :, nh:2 * nh], ALU.subtract).then_inc(s.d_ready, 1)
                if nh == 4:
                    V.tensor_tensor(m.rmax[:], m.rmax[:], lr, ALU.max).then_inc(s.ch, 1)
                take(v, s.ch, 4 if nh == 4 else 3)

            one_hot(0, 0)
            one_hot(1, 1)
            if nh:
                exponents(0, 0)

            def body(g, h, i):
                if exists(g + 2):
                    one_hot(g + 2, h + 2)
                if nh:
                    take(v, s.w_ready)
                    rows = m.ring[:, h, :, 0:D].rearrange("p j (n d) -> p j n d", n=nh)
                    w = bc(m.ring[:, h, :, D:D + nh].unsqueeze(3), (P, G, nh, D // nh))
                    V.tensor_tensor(rows, rows, w, ALU.mult).then_inc(s.msg_ready, 1)
                if weights is not None:
                    take(v, s.landed)
                    rows = m.ring[:, h, :, 0:width]
                    V.tensor_tensor(rows, rows, bc(weights[:, bass.ds(g * G, G)].unsqueeze(2), (P, G, width)),
                                    ALU.mult).then_inc(s.msg_ready, 1)
                if exists(g - 1):
                    add_up(g - 1, h - 1)
                if nh and exists(g + 1):
                    exponents(g + 1, h + 1)
            groups(v, body)
            add_up(NG - 1, R - 1)


def chunk(t, c, lo=0, hi=None):
    return t[:, bass.ds(c * CB, CB), lo:t.shape[2] if hi is None else hi]


def layer_norm(m, v, seq, dst, var_ready, std_ready):
    V = m.nc.vector
    mean, var, std, rstd = (m.st[:, k, :] for k in range(4))
    seq(V.tensor_reduce(mean, m.Y[:], AX, ALU.add))
    seq(V.tensor_scalar(mean, mean, -1.0 / D, None, ALU.mult))
    seq(V.tensor_tensor(m.Y[:], m.Y[:], bc(mean.unsqueeze(2), (P, CB, D)), ALU.add))
    seq(V.tensor_tensor(m.S[:], m.Y[:], m.Y[:], ALU.mult))
    seq(V.tensor_reduce(var, m.S[:], AX, ALU.add))
    V.tensor_scalar(var, var, 1.0 / D, EPS, ALU.mult, ALU.add).then_inc(var_ready, 1)
    take(v, std_ready)
    seq(V.reciprocal(rstd, std))
    return V.tensor_tensor(dst, m.Y[:], bc(rstd.unsqueeze(2), (P, CB, D)), ALU.mult)


def root(m, act, var_ready, std_ready):
    take(act, var_ready)
    m.nc.scalar.activation(m.st[:, 2, :], m.st[:, 1, :], ACT.Sqrt).then_inc(std_ready, 1)


def nodes_sage(m):
    nc = m.nc
    ch, mean_ok, tp, cp, mm, x_ok, vr, sr = (m.token(x) for x in (
        "ch", "mean", "transposed", "copied", "product", "x_ready", "var", "std"))
    o = m.sem("n0_stored")
    TP1 = m.PS[:, 0:2, :].rearrange("p k (j n) -> p (k j) n", j=4)
    TP2 = m.PS[:, 2:4, :].rearrange("p k (j n) -> p (k j) n", j=4)
    PO = m.PS[:, 4:6, :].rearrange("p k (j n) -> p (k j) n", j=4)
    with nc.Block() as block:
        @block.vector
        def _(v):
            V = nc.vector

            def seq(ins):
                ins.then_inc(ch, 1)
                take(v, ch)
            deg = m.rec[:, :, 0:1]
            seq(V.tensor_scalar(deg, m.A[:, :, D:D + 1], 1.0, None, ALU.max))
            seq(V.reciprocal(deg, deg))
            with v.Fori(0, NC) as c:
                V.tensor_copy(m.HR[:, :, 0:D], chunk(m.X, c)).then_inc(mean_ok, 1)
                V.tensor_tensor(m.M, chunk(m.A, c, 0, D), bc(chunk(m.rec, c, 0, 1), (P, CB, D)),
                                ALU.mult).then_inc(mean_ok, 1)
                take(v, mm)
                seq(V.tensor_tensor(m.Y[:], PO[:, 0:CB, :], chunk(m.X, c), ALU.add))
                layer_norm(m, v, seq, chunk(m.X, c), vr, sr).then_inc(x_ok, 1)

        @block.tensor
        def _(pe):
            with pe.Fori(0, NC) as c:
                take(pe, mean_ok, 2)
                for k in range(CB):
                    nc.tensor.transpose(TP1[:, k, :], m.HR[:, k, 0:D], m.ident[:])
                    t = nc.tensor.transpose(TP2[:, k, :], m.M[:, k, :], m.ident[:])
                t.then_inc(tp, 1)
                take(pe, cp, 2)
                for k in range(CB):
                    nc.tensor.matmul(PO[:, k, :], m.xT[:, k, :], m.w["self"][:], start=True, stop=False)
                    nc.tensor.matmul(PO[:, k, :], m.mT[:, k, :], m.w["neigh"][:], start=False, stop=False)
                    nc.tensor.matmul(PO[:, k, :], m.ones[0:1, :], m.bias[:, 0, :], start=False, stop=False)
                    t = nc.tensor.matmul(PO[:, k, :], m.ones[0:1, :], m.bias[:, 1, :], start=False, stop=True)
                t.then_inc(mm, 1)

        @block.scalar
        def _(act):
            with act.Fori(0, NC) as c:
                take(act, tp)
                nc.scalar.copy(m.xT, TP1[:, 0:CB, :]).then_inc(cp, 1)
                nc.scalar.copy(m.mT, TP2[:, 0:CB, :]).then_inc(cp, 1)
                root(m, act, vr, sr)

        @block.sync
        def _(sp):
            rows = m.tab1.rearrange("(b p) d -> p b d", p=P)
            with sp.Fori(0, NC) as c:
                take(sp, x_ok)
                sp.dma_start(rows[:, bass.ds(c * CB, CB), :], chunk(m.X, c)).then_inc(o, 16)
            sp.wait_ge(o, 16 * NC)


def nodes_project(m, tag, w, wa, nh, table, width, after_attention):
    nc = m.nc
    ch, x_ok, tp, cp, mm, h_ok, sc_ok, vr, sr, er, ed, mx, mxd, rows_free = (m.token(x) for x in (
        "ch", "x_ready", "transposed", "copied", "product", "h_ready", "sc_ready",
        "var", "std", "elu_in", "elu_out", "max_in", "max_out", "rows_free"))
    o = m.sem(tag + "_stored")
    TP1 = m.PS[:, 0:2, :].rearrange("p k (j n) -> p (k j) n", j=4)
    PO = m.PS[:, 4:6, :].rearrange("p k (j n) -> p (k j) n", j=4)
    PSC = m.PS[:, 6, 0:8 * CB].rearrange("p (j n) -> p j n", j=CB)
    with nc.Block() as block:
        @block.vector
        def _(v):
            V = nc.vector

            def seq(ins):
                ins.then_inc(ch, 1)
                take(v, ch)
            if after_attention:
                seq(V.tensor_reduce(m.gmax[:, 0:1], m.rmax[:].rearrange("p a b -> p (a b)"), AX, ALU.max))
                V.memset(m.tmp4[:], 0.0).then_inc(mx, 1)
                take(v, mxd)
                seq(V.tensor_scalar(m.tmp4[:], m.node[:, :, 4:8], m.gmax[:, 1:2], -1.0, ALU.subtract, ALU.mult))
                V.tensor_scalar(m.tmp4[:], m.tmp4[:], 0.0, None, ALU.add).then_inc(er, 1)
                take(v, ed)
                seq(V.scalar_tensor_tensor(out=m.rec[:], in0=m.tmp4[:], scalar=1e-8, in1=m.A[:, :, D:D + 4],
                                           op0=ALU.mult, op1=ALU.add))
                seq(V.reciprocal(m.rec[:], m.rec[:]))
            with v.Fori(0, NC) as c:
                x = chunk(m.X, c)
                if after_attention:
                    for j in range(4):
                        seq(V.tensor_tensor(m.M[:, :, 32 * j:32 * j + 32], chunk(m.A, c, 32 * j, 32 * j + 32),
                                            bc(chunk(m.rec, c, j, j + 1), (P, CB, 32)), ALU.mult))
                    V.tensor_scalar(m.S[:], m.M, 0.0, None, ALU.min).then_inc(er, 1)
                    take(v, ed)
                    seq(V.scalar_tensor_tensor(out=m.Y[:], in0=m.M, scalar=0.0, in1=m.S[:], op0=ALU.max, op1=ALU.add))
                    seq(V.scalar_tensor_tensor(out=m.Y[:], in0=m.Y[:], scalar=-1.0, in1=x, op0=ALU.add, op1=ALU.add))
                else:
                    seq(V.scalar_tensor_tensor(out=m.Y[:], in0=x, scalar=2.0, in1=chunk(m.A, c, 0, D),
                                               op0=ALU.mult, op1=ALU.add))
                layer_norm(m, v, seq, m.mT, vr, sr).then_inc(x_ok, 1)
                take(v, mm)
                seq(V.tensor_copy(chunk(m.nbr, c, 0, nh), PSC[:, :, 0:nh]))
                seq(V.tensor_copy(chunk(m.node, c, 0, nh), PSC[:, :, nh:2 * nh]))
                v.sem_inc(sc_ok)
            for j in range(nh):
                seq(V.tensor_reduce(m.gmax[:, j:j + 1], m.nbr[:, :, j], AX, ALU.max))
            v.sem_inc(mx)
            take(v, mxd)
            for j in range(nh):
                own, shift = m.node[:, :, j:j + 1], m.node[:, :, nh + j:nh + j + 1]
                seq(V.tensor_scalar(shift, own, m.sc[:, 0, 0, j:j + 1], None, ALU.add))
                seq(V.scalar_tensor_tensor(out=shift, in0=shift, scalar=SLOPE, in1=shift, op0=ALU.mult, op1=ALU.max))

        @block.gpsimd
        def _(pool):
            if after_attention:
                take(pool, mx)
                nc.gpsimd.partition_all_reduce(m.gmax[:, 1:2], m.gmax[:, 0:1], P, RMAX).then_inc(mxd, 1)
            take(pool, mx)
            nc.gpsimd.partition_all_reduce(m.sc[:, 0, 0, 0:nh], m.gmax[:, 0:nh], P, RMAX).then_inc(mxd, 1)

        @block.tensor
        def _(pe):
            with pe.Fori(0, NC) as c:
                take(pe, x_ok)
                for k in range(CB):
                    t = nc.tensor.transpose(TP1[:, k, :], m.mT[:, k, :], m.ident[:])
                t.then_inc(tp, 1)
                take(pe, cp, 2)
                for k in range(CB):
                    nc.tensor.matmul(PO[:, k, :], m.xT[:, k, :], w[:], start=True, stop=True)
                    t = nc.tensor.matmul(PSC[:, k, 0:2 * nh], m.xT[:, k, :], wa[:], start=True, stop=True)
                t.then_inc(h_ok, 1)

        @block.scalar
        def _(act):
            if after_attention:
                take(act, er)
                nc.scalar.activation(m.tmp4[:], m.tmp4[:], ACT.Exp).then_inc(ed, 1)

            with act.Fori(0, NC) as c:
                if after_attention:
                    take(act, er)
                    nc.scalar.activation(m.S[:], m.S[:], ACT.Exp).then_inc(ed, 1)
                root(m, act, vr, sr)
                take(act, tp)
                nc.scalar.copy(m.xT, TP1[:, 0:CB, :]).then_inc(cp, 1)
                nc.scalar.copy(chunk(m.X, c), m.mT).then_inc(cp, 1)
                take(act, h_ok)
                nc.scalar.copy(m.HR[:, :, 0:D], PO[:, 0:CB, :])
                nc.scalar.copy(m.HR[:, :, D:D + nh], PSC[:, :, 0:nh]).then_inc(mm, 1)
                take(act, rows_free)

        @block.sync
        def _(sp):
            rows = table.rearrange("(b p) d -> p b d", p=P)
            with sp.Fori(0, NC) as c:
                take(sp, sc_ok)
                sp.dma_start(rows[:, bass.ds(c * CB, CB), :], m.HR[:, :, 0:width]).then_inc(o, 16)
                sp.wait_ge(o, 16 * (c + 1))
                sp.sem_inc(rows_free)


def nodes_hop(m):
    nc = m.nc
    ch, ok, o = m.token("ch"), m.sem("n3_rows_ready"), m.sem("n3_stored")
    with nc.Block() as block:
        @block.vector
        def _(v):
            V = nc.vector

            def seq(ins):
                ins.then_inc(ch, 1)
                take(v, ch)
            den, r, t, u = m.A[:, :, D:D + 2], m.rec[:, :, 0:2], m.tmp4[:, :, 0:2], m.tmp4[:, :, 2:4]
            seq(V.tensor_scalar(t, den, 0.0, None, ALU.is_equal))
            seq(V.tensor_tensor(t, t, den, ALU.add))
            seq(V.reciprocal(r, t))
            seq(V.tensor_tensor(t, r, den, ALU.mult))
            seq(V.tensor_scalar(u, t, 0.0, None, ALU.is_equal))
            seq(V.tensor_tensor(u, u, t, ALU.add))
            seq(V.reciprocal(u, u))
            seq(V.tensor_tensor(r, r, u, ALU.mult))
            for i in (1, 0):
                rows = m.A[:, :, 64 * i:64 * i + 64]
                V.tensor_tensor(rows, rows, bc(m.rec[:, :, i:i + 1], (P, NB, 64)), ALU.mult).then_inc(ok, 1)

        @block.sync
        def _(sp):
            sp.wait_ge(ok, 1)
            sp.dma_start(m.tab4.rearrange("(b p) d -> p b d", p=P), m.A[:, :, 64:128]).then_inc(o, 16)
            sp.wait_ge(o, 16)


def nodes_final(m):
    nc = m.nc
    ch, gi_, go, ok, vr, sr = (m.token(x) for x in ("ch", "elu_in", "elu_out", "x_ready", "var", "std"))
    o = m.sem("n4_stored")
    with nc.Block() as block:
        @block.vector
        def _(v):
            V = nc.vector

            def seq(ins):
                ins.then_inc(ch, 1)
                take(v, ch)
            full = (P, CB, D)
            with v.Fori(0, NC) as c:
                seq(V.tensor_scalar(m.Y[:, :, 0:64], chunk(m.A, c, 0, 64), 0.0, None, ALU.add))
                seq(V.tensor_tensor(m.Y[:, :, 64:128], chunk(m.A, c, 64, 128), bc(chunk(m.rec, c, 1, 2), (P, CB, 64)), ALU.mult))
                seq(V.tensor_tensor(m.xT.bitcast(I32), m.Y[:], m.Y[:], ALU.is_equal))
                seq(V.memset(m.M, 0.0))
                seq(V.copy_predicated(m.M, m.xT.bitcast(I32), m.Y[:]))
                seq(V.tensor_tensor(m.M, m.M, bc(m.w["b3"][:].unsqueeze(1), full), ALU.add))
                seq(V.tensor_tensor(m.S[:], m.M, bc(m.w["fc3"][:].unsqueeze(1), full), ALU.mult))
                seq(V.tensor_reduce(m.gg[:], m.S[:].rearrange("p b (i d) -> p b i d", i=2), AX, ALU.add))
                V.tensor_tensor(m.gg[:], m.gg[:], bc(m.bf3[:].unsqueeze(1), (P, CB, 2)), ALU.add).then_inc(gi_, 1)
                take(v, go)
                seq(V.tensor_scalar(m.gg[:], m.gg[:], 1.0, None, ALU.add))
                seq(V.reciprocal(m.gg[:], m.gg[:]))
                seq(V.tensor_scalar(m.S[:], m.M, 0.0, None, ALU.min))
                for i in range(2):
                    h = m.S[:, :, 64 * i:64 * i + 64]
                    seq(V.tensor_tensor(h, h, bc(m.gg[:, :, i:i + 1], (P, CB, 64)), ALU.mult))
                seq(V.scalar_tensor_tensor(out=m.M, in0=m.M, scalar=0.0, in1=m.S[:], op0=ALU.max, op1=ALU.add))
                seq(V.scalar_tensor_tensor(out=m.M, in0=m.M, scalar=SLOPE, in1=m.M, op0=ALU.mult, op1=ALU.max))
                seq(V.tensor_tensor(m.Y[:], m.M, chunk(m.X, c), ALU.add))
                seq(layer_norm(m, v, seq, chunk(m.X, c), vr, sr))
                v.sem_inc(ok)

        @block.scalar
        def _(act):
            with act.Fori(0, NC) as c:
                take(act, gi_)
                nc.scalar.activation(m.gg[:], m.gg[:], ACT.Exp, scale=-1.0).then_inc(go, 1)
                root(m, act, vr, sr)

        @block.sync
        def _(sp):
            full = (NB - 1) * P
            rows = m.out[0:full, :].rearrange("(b p) d -> p b d", p=P)
            with sp.Fori(0, NC - 1) as c:
                take(sp, ok)
                sp.dma_start(rows[:, bass.ds(c * CB, CB), :], chunk(m.X, c)).then_inc(o, 16)
            take(sp, ok)
            b = (NC - 1) * CB
            sp.dma_start(rows[:, b:NB - 1, :], m.X[:, b:NB - 1, :]).then_inc(o, 16)
            sp.dma_start(m.out[full:N, :], m.X[0:LAST, NB - 1, :]).then_inc(o, 16)
            sp.wait_ge(o, 16 * (NC + 1))


NAMES = ["x", "src", "dst", "edge_attr_128", "L0_gnn_W_self", "L0_gnn_b_self", "L0_gnn_W_neigh", "L0_gnn_b_neigh",
         "L2_gnn_W", "L2_gnn_A_left", "L2_gnn_A_right", "L3_gnn_W", "L3_gnn_b", "L3_gnn_fc", "L3_gnn_bf",
         "L3_gnn_a_src", "L3_gnn_a_dst"]


def kernel(**inputs):
    import numpy as np
    import concourse.bacc as bacc
    from concourse.bass_utils import run_bass_kernel_spmd

    nc = bacc.Bacc("TRN2", target_bir_lowering=False, num_devices=1)
    arrays, aps = {}, {}
    for name in NAMES:
        arr = np.ascontiguousarray(inputs[name])
        arrays["in_" + name] = arr
        aps[name] = nc.dram_tensor("in_" + name, arr.shape, mybir.dt.from_np(arr.dtype), kind="ExternalInput").ap()
    out = nc.dram_tensor("out_0", (N, D), F32, kind="ExternalOutput").ap()
    build(nc, aps, out)
    r = run_bass_kernel_spmd(nc, [arrays], core_ids=[0])
    return r.results[0]["out_0"]
```

```python
from contextlib import ExitStack

import concourse.bass as bass
from concourse import mybir
from concourse.alu_op_type import AluOpType as ALU

ACT = mybir.ActivationFunctionType
F32 = mybir.dt.float32
I32 = mybir.dt.int32
AX = mybir.AxisListType.X
RMAX = bass.bass_isa.ReduceOp.max

P = 128
D = 128
N = 12500
E = 200000
NB = -(-N // P)
LAST = N - (NB - 1) * P
EP = 125
EC = E // EP
G = 4
R = 4
TD = E // EP
T = -(-max((E + NB * (P - 1)) // P, TD + NB) // (R * G)) * (R * G)
NG = T // G
CB = 7
NC = NB // CB
RW = 132
NO_ROW = NB * P - 1
NO_NODE = 255
EPS = 1e-5
SLOPE = 0.2


class Parts:
    pass


def take(eng, sem, n=1):
    eng.wait_ge(sem, n).then_inc(sem, -n)


def bc(ap, shape):
    return ap.broadcast_to(list(shape))


def build(nc, a, out):
    with ExitStack() as ctx:
        def sb(name, shape, dt=F32):
            return ctx.enter_context(nc.sbuf_tensor(name, shape, dt))

        m = Parts()
        m.nc, m.a, m.out = nc, a, out
        m.sem = lambda name: ctx.enter_context(nc.semaphore(name))
        tokens = {}

        def token(name):
            if name not in tokens:
                tokens[name] = m.sem(name)
            return tokens[name]
        m.token = token

        def dram(name, shape, dt=F32):
            return nc.dram_tensor(name, shape, dt).ap()
        m.rec_src = dram("rec_by_src", (P * T, 4), I32)
        m.rec_dst = dram("rec_by_dst", (E, 2), I32)
        m.src_g, m.dst_g = dram("src_sorted", (E,), I32), dram("dst_sorted", (E,), I32)
        m.attr_g = dram("attr_sorted", (E, D))
        m.tab1 = dram("x1_rows", (NB * P, D))
        m.tab2 = dram("h2_rows", (NB * P, RW))
        m.tab3 = dram("h3_rows", (NB * P, D + 2))
        m.tab4 = dram("hop_rows", (NB * P, 64))

        m.X = sb("X", [P, NB, D])
        m.A = sb("A", [P, NB, RW])
        m.gi_d, m.gi_s = sb("gi_d", [P, T], I32), sb("gi_s", [P, T], I32)
        m.w1 = sb("w1", [P, T])
        m.tile_of = m.w1[0:1, :].bitcast(I32)
        m.unsorted = sb("unsorted", [1, 1], I32)
        m.li_d, m.li_s = sb("li_d", [P, T]), sb("li_s", [P, T])
        m.low = sb("low", [1, 4])
        m.bt_d, m.bt_s = sb("bt_d", [1, NG], I32), sb("bt_s", [1, NG], I32)
        m.ring = sb("ring", [P, R, G, RW])
        m.ring2 = sb("ring2", [P, R, G, D])
        m.idx = sb("idx", [P, R, G], I32)
        m.oh = sb("oh", [P, R, G, P])
        m.ohT = sb("ohT", [P, 2, G, P])
        m.sc = sb("sc", [P, 2, G, 4])
        m.lr = sb("lr", [P, 2, G, 4])
        m.dd = sb("dd", [P, 2, G, 4])
        m.rmax = sb("rmax", [P, G, 4])
        m.gmax = sb("gmax", [P, 4])
        m.node = sb("node", [P, NB, 8])
        m.nbr = sb("nbr", [P, NB, 4])
        m.rec = sb("rec", [P, NB, 4])
        m.tmp4 = sb("tmp4", [P, NB, 4])
        m.iota = sb("iota", [P, P])
        m.pidx = sb("pidx", [P, 1])
        m.ident = sb("ident", [P, P])
        m.tri = sb("tri", [P, P])
        m.ones = sb("ones", [P, P])
        m.iota_b = sb("iota_b", [P, NB])
        m.w = {n: sb("w_" + n, [P, D]) for n in ("self", "neigh", "l2", "l3", "t1", "b3", "fc3")}
        m.wa2, m.wa3 = sb("wa2", [P, 8]), sb("wa3", [P, 4])
        m.bd = sb("bd", [P, 12])
        m.bias = sb("bias", [2, D])
        m.bf3 = sb("bf3", [P, 2])
        m.Y = sb("Y", [P, CB, D])
        m.S = sb("S", [P, CB, D])
        ring_view = lambda t, k: t[:].rearrange("p h j n -> p (h j) n")[:, 8 * k:8 * k + CB, 0:D]
        m.M2, m.mT2, m.xT2 = ([ring_view(t, k) for k in range(2)] for t in (m.oh, m.ring2, m.ring))
        m.M, m.xT = m.M2[0], m.xT2[0]
        m.xc2 = [ring_view(m.ohT, 0), sb("xc", [P, CB, D])[:]]
        m.HR = sb("HR", [P, 2, CB, RW])
        m.st = sb("st", [P, 4, CB])
        m.gg = sb("gg", [P, CB, 2])
        m.PS = ctx.enter_context(nc.psum_tensor("PS", [P, 8, 512], F32))

        prepare(m)
        list_tiles(m)
        sort_edges(m)
        group_by_source(m)
        load_nodes(m)
        edge_pass(m, "e0", a["x"], D, m.gi_d, m.li_d, m.bt_d, 0, D + 1, ones=True)
        nodes_sage(m)
        edge_pass(m, "e1", m.tab1, D, m.gi_d, m.li_d, m.bt_d, 0, D, attr=True)
        nodes_project(m, "n1", m.w["l2"], m.wa2, 4, m.tab2, D + 4, after_attention=False)
        edge_pass(m, "e2", m.tab2, D + 4, m.gi_s, m.li_s, m.bt_s, 0, D + 4, heads=4)
        nodes_project(m, "n2", m.w["l3"], m.wa3, 2, m.tab3, D + 2, after_attention=True)
        edge_pass(m, "e3", m.tab3, D + 2, m.gi_s, m.li_s, m.bt_s, 0, D + 2, heads=2)
        nodes_hop(m)
        edge_pass(m, "e4", m.tab4, 64, m.gi_s, m.li_s, m.bt_s, 64, 64, weights=m.w1)
        nodes_final(m)


def prepare(m):
    nc, a = m.nc, m.a
    loaded, made, step = m.sem("w_loaded"), m.sem("const_made"), m.sem("w_step")
    pe_done, copied, zeroed = m.sem("w_pe"), m.sem("w_copied"), m.sem("w_zeroed")
    n_loads = 10 + 8 + 4
    with nc.Block() as block:
        @block.sync
        def _(sp):
            sp.dma_start(m.w["self"][:], a["L0_gnn_W_self"]).then_inc(loaded, 16)
            sp.dma_start(m.w["neigh"][:], a["L0_gnn_W_neigh"]).then_inc(loaded, 16)
            sp.dma_start(m.w["l2"][:], a["L2_gnn_W"]).then_inc(loaded, 16)
            for i in range(2):
                sp.dma_start(m.w["l3"][:, 64 * i:64 * i + 64], a["L3_gnn_W"][i]).then_inc(loaded, 16)
            sp.dma_start(m.bias[0:1, :], a["L0_gnn_b_self"].rearrange("(o d) -> o d", o=1)).then_inc(loaded, 16)
            sp.dma_start(m.bias[1:2, :], a["L0_gnn_b_neigh"].rearrange("(o d) -> o d", o=1)).then_inc(loaded, 16)
            sp.dma_start(m.w["b3"][:], a["L3_gnn_b"].rearrange("i d -> (i d)").partition_broadcast(P)).then_inc(loaded, 16)
            sp.dma_start(m.w["fc3"][:], a["L3_gnn_fc"].rearrange("i d o -> (i d o)").partition_broadcast(P)).then_inc(loaded, 16)
            sp.dma_start(m.bf3[:], a["L3_gnn_bf"].partition_broadcast(P)).then_inc(loaded, 16)
            sp.wait_ge(zeroed, 1)
            for h in range(4):
                sp.dma_start(m.bd[32 * h:32 * h + 32, h:h + 1], a["L2_gnn_A_right"][h]).then_inc(loaded, 16)
                sp.dma_start(m.bd[32 * h:32 * h + 32, 4 + h:5 + h], a["L2_gnn_A_left"][h]).then_inc(loaded, 16)
            for i in range(2):
                for col, name in ((8, "L3_gnn_a_dst"), (10, "L3_gnn_a_src")):
                    sp.dma_start(m.bd[64 * i:64 * i + 64, col + i:col + i + 1],
                                 a[name][i].rearrange("(d o) -> d o", o=1)).then_inc(loaded, 16)

        @block.gpsimd
        def _(pool):
            kw = dict(allow_small_or_imprecise_dtypes=True)
            nc.gpsimd.iota(m.iota[:], [[1, P]], base=0, channel_multiplier=0, **kw).then_inc(made, 1)
            nc.gpsimd.iota(m.pidx[:], [[0, 1]], base=0, channel_multiplier=1, **kw).then_inc(made, 1)
            nc.gpsimd.iota(m.iota_b[:], [[1, NB]], base=0, channel_multiplier=0, **kw).then_inc(made, 1)
            nc.gpsimd.memset(m.ones[:], 1.0).then_inc(made, 1)

        @block.vector
        def _(v):
            nc.vector.memset(m.low[:], -1e30)
            nc.vector.memset(m.bd[:], 0.0).then_inc(zeroed, 1)
            v.wait_ge(made, 4)
            nc.vector.tensor_scalar(m.ident[:], m.iota[:], m.pidx[:], None, ALU.is_equal).then_inc(step, 1)
            nc.vector.tensor_scalar(m.tri[:], m.iota[:], m.pidx[:], None, ALU.is_gt).then_inc(step, 1)
            v.wait_ge(loaded, 16 * n_loads)
            v.wait_ge(pe_done, 1)
            nc.vector.tensor_copy(m.w["self"][:], m.PS[:, 0, 0:D]).then_inc(copied, 1)
            nc.vector.tensor_copy(m.w["neigh"][:], m.PS[:, 1, 0:D]).then_inc(copied, 1)
            nc.vector.tensor_copy(m.w["t1"][:], m.PS[:, 2, 0:D]).then_inc(copied, 1)
            nc.vector.tensor_copy(m.M[:, 0, :], m.PS[:, 3, 0:D]).then_inc(copied, 1)
            v.wait_ge(pe_done, 2)
            nc.vector.tensor_copy(m.wa2[:], m.PS[:, 4, 0:8]).then_inc(copied, 1)
            nc.vector.tensor_copy(m.wa3[:], m.PS[:, 5, 0:4]).then_inc(copied, 1)

        @block.tensor
        def _(pe):
            pe.wait_ge(loaded, 16 * n_loads)
            pe.wait_ge(step, 2)
            for k, name in enumerate(("self", "neigh", "l2", "l3")):
                t = nc.tensor.transpose(m.PS[:, k, 0:D], m.w[name][:], m.ident[:])
            t.then_inc(pe_done, 1)
            pe.wait_ge(copied, 4)
            nc.tensor.matmul(m.PS[:, 4, 0:8], m.w["t1"][:], m.bd[:, 0:8], start=True, stop=True)
            nc.tensor.matmul(m.PS[:, 5, 0:4], m.M[:, 0, :], m.bd[:, 8:12], start=True, stop=True).then_inc(pe_done, 1)


def steps(m, eng, sem):
    def step(ins):
        ins.then_inc(sem, 1)
        take(eng, sem)
    return step


def edge_words(m):
    w = Parts()
    A = m.A[:].rearrange("p b w -> p (b w)")
    X = m.X[:].rearrange("p b w -> p (b w)")
    AI, XI = A.bitcast(I32), X.bitcast(I32)
    w.recs = AI[0:EP, 0:4 * EC].rearrange("p (c w) -> p c w", w=4)
    w.pairs = AI[0:EP, 0:2 * EC].rearrange("p (c w) -> p c w", w=2)
    w.apart = [AI[0:EP, (2 + k) * EC:(3 + k) * EC] for k in range(2)]
    w.back = AI[:, 0:4 * T].rearrange("p (t w) -> p t w", w=4)
    w.key = AI[0:EP, 5 * EC:6 * EC]
    w.masks = [AI[0:EP, k * EC:(k + 1) * EC] for k in (2, 3, 6)]
    w.runs = [A[0:EP, k * EC:(k + 1) * EC] for k in (4, 7)]
    w.pos, w.row, w.other, w.hi = X[0:EP, 0:EC], XI[0:EP, EC:2 * EC], XI[0:EP, 2 * EC:3 * EC], XI[0:EP, 3 * EC:4 * EC]
    w.zero, w.blk = X[0:EP, 4 * EC:5 * EC], X[0:EP, 5 * EC:6 * EC]
    x = 6 * EC
    w.turn = m.st[:, 0, :]
    w.fill = XI[:, x:x + 64].rearrange("p (t w) -> p t w", w=4)
    w.cnt, w.tiles, w.incl, w.base, w.none, w.start = (
        X[:, x + 64 + k * NB:x + 64 + (k + 1) * NB] for k in range(6))
    w.tiles_i = XI[:, x + 64 + 6 * NB:x + 64 + 7 * NB]
    w.col = X[0:NB, x + 64 + 7 * NB:x + 80 + 7 * NB]
    w.iota_all, w.iota_t, w.cmp, w.cmp2 = X[:, 0:T], X[0:NB, 0:T], X[0:NB, 2 * EC:2 * EC + T], X[0:NB, 4 * EC:4 * EC + T]
    w.row_i = AI[0:1, 0:T]
    w.picks = X[:, 2 * EC:6 * EC]
    assert x + 80 + 7 * NB <= NB * D and T <= 2 * EC and 8 * EC <= NB * RW and 4 * T <= 5 * EC
    return w


def count_blocks(m, v, w, counted, cnt):
    v.sem_inc(counted, 2)
    with v.Fori(0, NB // 2) as i:
        for h in range(2):
            b = 2 * i + h
            take(v, counted)
            m.nc.vector.tensor_scalar(w.runs[h], w.blk, m.iota_b[0:EP, bass.ds(b, 1)], None, ALU.is_equal, ALU.add,
                                      accum_out=cnt[0:EP, bass.ds(b, 1)]).then_inc(counted, 1)
    take(v, counted, 2)


RANK_TURN = 6


def block_masks(m, pool, w, mask_free, mask_ready, numbered):
    def mask(k):
        block = w.turn[0:EP, k:k + 1]
        take(pool, mask_free)
        m.nc.gpsimd.tensor_scalar(block, block, float(RANK_TURN), None, ALU.add).then_inc(numbered, 1)
        take(pool, numbered)
        m.nc.gpsimd.tensor_scalar(w.masks[k % 3], w.blk, block, None, ALU.is_equal).then_inc(mask_ready, 1)
    with pool.Fori(0, NB // RANK_TURN):
        for k in range(RANK_TURN):
            mask(k)
    for k in range(NB % RANK_TURN):
        mask(k)


def rank_edges(m, v, w, step, mask_free, mask_ready, scanned, copied, started):
    V = m.nc.vector
    step(V.tensor_scalar(w.turn[0:EP, 0:RANK_TURN], m.iota_b[0:EP, 0:RANK_TURN], -float(RANK_TURN), None, ALU.add))
    v.sem_inc(mask_free, 2)
    step(V.memset(w.pos, 0.0))

    def start(b, k):
        return V.tensor_copy(w.start[0:EP, k % 2:k % 2 + 1], w.base[0:EP, bass.ds(b, 1)])

    def scan(k):
        take(v, mask_ready)
        V.tensor_tensor_scan(w.runs[k % 2], w.masks[k % 3], w.zero, w.start[0:EP, k % 2:k % 2 + 1],
                             ALU.add, ALU.add).then_inc(scanned, 1)

    def choose(b, k):
        take(v, copied)
        if not isinstance(b, int):
            v.sem_inc(mask_free)
        if not isinstance(b, int) or b + 1 < NB:
            take(v, started)
            scan(k + 1)
        take(v, scanned)
        V.copy_predicated(w.pos, w.masks[k % 3], w.runs[k % 2]).then_inc(copied, 1)
        if not isinstance(b, int) or b + 2 < NB:
            start(b + 2, k).then_inc(started, 1)

    step(start(0, 0))
    start(1, 1).then_inc(started, 1)
    scan(0)
    v.sem_inc(copied)
    last = NB - NB % RANK_TURN
    with v.Fori(0, NB // RANK_TURN) as i:
        for k in range(RANK_TURN):
            choose(i * RANK_TURN + k, k)
    for b in range(last, NB):
        choose(b, b)
    take(v, copied)


def pack_blocks(m, step, row_i, bt):
    V = m.nc.vector
    four = row_i.rearrange("o (g j) -> o g j", j=G)
    step(V.tensor_copy(bt[:], four[:, :, 0]))
    for j in range(1, G):
        step(V.tensor_scalar(four[:, :, j], four[:, :, j], 7 * j, None, ALU.logical_shift_left))
        step(V.tensor_tensor(bt[:], bt[:], four[:, :, j], ALU.bitwise_or))


def list_tiles(m):
    nc = m.nc
    w = edge_words(m)
    counted = m.token("counted")
    q = T // 4
    loaded, made, ok, pe_ok = (m.sem("lt_" + x) for x in ("loaded", "iota", "vector", "tensor"))
    tot, s, f, l, n, st, inc, delta, minus, has = (w.col[:, k:k + 1] for k in range(10))
    delta_all, minus_all = m.M[0:NB, 0, :], m.M[0:NB, 1, :]
    place_tile = m.gi_s[:].bitcast(F32)
    with nc.Block() as block:
        @block.sync
        def _(sp):
            sp.dma_start(w.key, m.a["dst"].rearrange("(p c) -> p c", c=EC)).then_inc(loaded, 16)
            sp.dma_start(w.other[0:EP - 1, :], m.a["dst"][1:1 + (EP - 1) * EC].rearrange("(p c) -> p c", c=EC)).then_inc(loaded, 16)
            sp.dma_start(w.other[EP - 1:EP, 0:EC - 1], m.a["dst"][(EP - 1) * EC + 1:E].rearrange("(p c) -> p c", p=1)).then_inc(loaded, 16)
            sp.dma_start(w.other[EP - 1:EP, EC - 1:EC], m.a["dst"][E - 1:E].rearrange("(p c) -> p c", p=1)).then_inc(loaded, 16)

        @block.gpsimd
        def _(pool):
            kw = dict(allow_small_or_imprecise_dtypes=True)
            nc.gpsimd.iota(w.iota_all, [[1, T]], base=0, channel_multiplier=0, **kw).then_inc(made, 1)
            nc.gpsimd.iota(m.ring[:].rearrange("p r g n -> p (r g n)")[0:NB, 0:TD], [[EP, TD]], base=EP,
                           channel_multiplier=0, **kw).then_inc(made, 1)

        firsts = m.ring[:].rearrange("p r g n -> p (r g n)")[0:NB, 0:TD]

        @block.tensor
        def _(pe):
            ones = m.ones
            pe.wait_ge(ok, 1)
            nc.tensor.matmul(m.PS[0:NB, 0, 0:1], w.cnt[0:EP, :], ones[0:EP, 0:1], start=True, stop=True)
            nc.tensor.matmul(m.PS[0:1, 7, 0:1], w.tiles[0:EP, 0:1], ones[0:EP, 0:1], start=True, stop=True).then_inc(pe_ok, 1)
            pe.wait_ge(ok, 2)
            nc.tensor.matmul(m.PS[0:NB, 1, 0:1], m.tri[0:NB, 0:NB], tot, start=True, stop=True).then_inc(pe_ok, 1)
            pe.wait_ge(ok, 3)
            nc.tensor.matmul(m.PS[0:NB, 2, 0:1], m.tri[0:NB, 0:NB], n, start=True, stop=True).then_inc(pe_ok, 1)
            pe.wait_ge(ok, 4)
            for k in range(4):
                t = nc.tensor.matmul(m.PS[:, k, 0:q], ones[0:NB, :], w.cmp[:, q * k:q * k + q], start=True, stop=True)
            t.then_inc(pe_ok, 1)
            for k in range(4):
                nc.tensor.matmul(m.PS[:, 4 + k, 0:q], delta_all, w.cmp2[:, q * k:q * k + q], start=True, stop=False)
                t = nc.tensor.matmul(m.PS[:, 4 + k, 0:q], minus_all, w.cmp[:, q * k:q * k + q], start=False, stop=True)
            t.then_inc(pe_ok, 1)

        @block.vector
        def _(v):
            V = nc.vector
            step = steps(m, v, m.token("ch"))
            step(V.memset(w.cnt, 0.0))
            v.wait_ge(loaded, 64)
            step(V.tensor_scalar(w.hi, w.key, 7, None, ALU.logical_shift_right))
            step(V.tensor_copy(w.blk, w.hi))
            step(V.tensor_tensor(w.runs[0], w.other, w.key, ALU.is_lt))
            step(V.tensor_reduce(w.tiles[0:EP, 0:1], w.runs[0], AX, ALU.add))
            count_blocks(m, v, w, counted, w.cnt)
            v.sem_inc(ok)
            v.wait_ge(pe_ok, 1)
            step(V.tensor_scalar(m.unsorted[:], m.PS[0:1, 7, 0:1], 1.0, None, ALU.min))
            step(V.tensor_copy(tot, m.PS[0:NB, 0, 0:1]))
            v.sem_inc(ok)
            v.wait_ge(pe_ok, 2)
            v.wait_ge(made, 2)
            step(V.tensor_copy(s, m.PS[0:NB, 1, 0:1]))
            step(V.tensor_tensor(l, s, tot, ALU.add))
            step(V.tensor_scalar(l, l, -1.0, None, ALU.add))
            step(V.tensor_scalar(w.cmp[:, 0:TD], firsts, s, None, ALU.is_le))
            step(V.tensor_reduce(f, w.cmp[:, 0:TD], AX, ALU.add))
            step(V.tensor_scalar(w.cmp[:, 0:TD], firsts, l, None, ALU.is_le))
            step(V.tensor_reduce(l, w.cmp[:, 0:TD], AX, ALU.add))
            step(V.tensor_tensor(n, l, f, ALU.subtract))
            step(V.tensor_scalar(has, tot, 0.0, None, ALU.is_gt))
            step(V.scalar_tensor_tensor(out=n, in0=n, scalar=1.0, in1=has, op0=ALU.add, op1=ALU.mult))
            v.sem_inc(ok)
            v.wait_ge(pe_ok, 3)
            step(V.tensor_copy(st, m.PS[0:NB, 2, 0:1]))
            step(V.tensor_tensor(inc, st, n, ALU.add))
            step(V.tensor_tensor(delta, f, st, ALU.subtract))
            step(V.tensor_scalar(minus, delta, -1.0, None, ALU.mult))
            step(V.tensor_scalar(delta_all, m.ones[0:NB, :], delta, None, ALU.mult))
            step(V.tensor_scalar(minus_all, m.ones[0:NB, :], minus, None, ALU.mult))
            step(V.tensor_scalar(w.cmp, w.iota_t, inc, None, ALU.is_ge))
            step(V.tensor_scalar(w.cmp2, w.iota_t, st, None, ALU.is_ge))
            v.sem_inc(ok)
            v.wait_ge(pe_ok, 4)
            step(V.tensor_scalar(w.cnt[:, 0:1], m.pidx[:], float(EP), 1e6, ALU.is_ge, ALU.mult))
            for k in range(4):
                at = slice(q * k, q * k + q)
                step(V.tensor_scalar(m.li_d[:, at], m.PS[:, k, 0:q], float(P), w.cnt[:, 0:1], ALU.mult, ALU.add))
                step(V.tensor_scalar(w.row_i[:, at], m.PS[0:1, k, 0:q], float(NB - 1), None, ALU.min))
            pack_blocks(m, step, w.row_i, m.bt_d)
            v.wait_ge(pe_ok, 5)
            for k in range(4):
                at = slice(q * k, q * k + q)
                step(V.tensor_tensor(place_tile[:, at], m.PS[:, 4 + k, 0:q], w.iota_all[:, at], ALU.add))
            step(V.tensor_scalar(m.tile_of, place_tile[0:1, :], float(TD - 1), None, ALU.min))
            step(V.memset(m.gi_d[:], 0))


def sort_edges(m):
    nc = m.nc
    w = edge_words(m)
    counted = m.token("counted")
    turns = mask_free, mask_ready, *_ = [m.token(x) for x in ("mask_free", "mask_ready", "scanned", "copied", "started")]
    NGE = EC // G
    loaded, ok, pe_ok, back, out = (m.sem("so_" + x) for x in ("loaded", "vector", "tensor", "back", "out"))
    ring_ok, seen = m.token("scatter_ring"), m.token("scatter_seen")
    features_ok = m.token("features_landed")
    scattered = [m.sem(f"so_sc{h}") for h in range(2)]
    pring = m.ring[:].bitcast(I32)
    attr = m.a["edge_attr_128"].rearrange("(p c) d -> p c d", c=EC)

    def branch(eng, general, plain=None):
        unsorted = eng.value_load(m.unsorted[:], min_val=0, max_val=1)
        with eng.If_ne(eng.to_reg(unsorted), 0):
            general()
        with eng.Else():
            if plain:
                plain()
            else:
                eng.nop()
        eng.drain()

    with nc.Block() as block:
        @block.sync
        def _(sp):
            def general():
                sp.dma_start(w.key, m.a["dst"].rearrange("(p c) -> p c", c=EC)).then_inc(loaded, 16)
                sp.dma_start(w.other, m.a["src"].rearrange("(p c) -> p c", c=EC)).then_inc(loaded, 16)
                for h in range(2):
                    sp.wait_ge(scattered[h], 32 * G)
                    sp.sem_inc(seen)
                with sp.Fori(1, NGE // 2) as i:
                    for h in range(2):
                        sp.wait_ge(scattered[h], 32 * G * (i + 1))
                        sp.sem_inc(seen)
                sp.dma_start(w.pairs, m.rec_dst.rearrange("(p c) w -> p c w", c=EC)).then_inc(back, 16)
                sp.wait_ge(ok, 3)
                sp.dma_start(m.src_g.rearrange("(p c) -> p c", c=EC), w.apart[0]).then_inc(out, 16)
                sp.dma_start(m.dst_g.rearrange("(p c) -> p c", c=EC), w.apart[1]).then_inc(out, 16)
                sp.wait_ge(out, 32)

            def plain():
                sp.dma_start(m.src_g.rearrange("(p c) -> p c", c=EC), m.a["src"].rearrange("(p c) -> p c", c=EC)).then_inc(out, 16)
                sp.dma_start(m.dst_g.rearrange("(p c) -> p c", c=EC), m.a["dst"].rearrange("(p c) -> p c", c=EC)).then_inc(out, 16)
                sp.wait_ge(out, 32)
            branch(sp, general, plain)

        @block.gpsimd
        def _(pool):
            def general():
                block_masks(m, pool, w, mask_free, mask_ready, m.token("numbered"))
                with pool.Fori(0, NGE // 2) as i:
                    for h in range(2):
                        take(pool, ring_ok)
                        take(pool, features_ok)
                        for j in range(G):
                            at = bass.IndirectOffsetOnAxis(ap=m.idx[0:EP, h, j:j + 1], axis=0)
                            nc.gpsimd.indirect_dma_start(out=m.rec_dst, out_offset=at, in_=pring[0:EP, h, j, 0:2],
                                                         in_offset=None).then_inc(scattered[h], 16)
                            nc.gpsimd.indirect_dma_start(out=m.attr_g, out_offset=at, in_=m.ring2[0:EP, h, j, :],
                                                         in_offset=None).then_inc(scattered[h], 16)
            branch(pool, general)

        @block.scalar
        def _(act):
            f_in = m.sem("so_features")

            def general():
                act.wait_ge(ok, 2)

                def fill(g, h, n):
                    for j in range(G):
                        act.dma_start(m.ring2[0:EP, h, j, :],
                                      attr[:, bass.ds(g * G + j, 1), :].rearrange("p o d -> p (o d)")).then_inc(f_in, 16)
                    nc.scalar.copy(m.idx[0:EP, h, :], w.row[:, bass.ds(g * G, G)])
                    nc.scalar.copy(pring[0:EP, h, :, 0:2], w.pairs[:, bass.ds(g * G, G), :]).then_inc(ring_ok, 1)
                    act.wait_ge(f_in, n)
                    act.sem_inc(features_ok)
                fill(0, 0, 16 * G)
                fill(1, 1, 32 * G)
                with act.Fori(1, NGE // 2) as i:
                    for h in range(2):
                        take(act, seen)
                        fill(2 * i + h, h, (2 * i + h + 1) * (16 * G))
                take(act, seen, 2)
            branch(act, general)

        @block.tensor
        def _(pe):
            def general():
                pe.wait_ge(ok, 1)
                nc.tensor.matmul(m.PS[:, 0, 0:NB], m.ones[0:EP, :], w.cnt[0:EP, :], start=True, stop=True)
                nc.tensor.matmul(m.PS[:, 1, 0:NB], m.tri[0:EP, :], w.cnt[0:EP, :], start=True, stop=True).then_inc(pe_ok, 1)
            branch(pe, general)

        @block.vector
        def _(v):
            V = nc.vector
            step = steps(m, v, m.token("ch"))

            def general():
                step(V.memset(w.cnt, 0.0))
                step(V.memset(w.zero, 0.0))
                step(V.memset(w.none, 0.0))
                v.wait_ge(loaded, 32)
                step(V.tensor_scalar(w.hi, w.key, 7, None, ALU.logical_shift_right))
                step(V.tensor_copy(w.blk, w.hi))
                step(V.tensor_copy(w.pairs[:, :, 0], w.other))
                step(V.tensor_copy(w.pairs[:, :, 1], w.key))
                count_blocks(m, v, w, counted, w.cnt)
                v.sem_inc(ok)
                v.wait_ge(pe_ok, 1)
                step(V.tensor_copy(w.tiles, m.PS[:, 0, 0:NB]))
                step(V.tensor_tensor_scan(w.incl, w.tiles, w.none, -1.0, ALU.add, ALU.add))
                step(V.tensor_tensor(w.base, w.incl, w.tiles, ALU.subtract))
                step(V.tensor_tensor(w.base, w.base, m.PS[:, 1, 0:NB], ALU.add))
                rank_edges(m, v, w, step, *turns)
                step(V.tensor_copy(w.row, w.pos))
                v.sem_inc(ok)
                v.wait_ge(back, 16)
                step(V.tensor_copy(w.apart[0], w.pairs[:, :, 0]))
                step(V.tensor_copy(w.apart[1], w.pairs[:, :, 1]))
                v.sem_inc(ok)
            branch(v, general)


def group_by_source(m):
    nc = m.nc
    w = edge_words(m)
    counted = m.token("counted")
    turns = mask_free, mask_ready, *_ = [m.token(x) for x in ("mask_free", "mask_ready", "scanned", "copied", "started")]
    NGE = EC // G
    q = T // 4
    loaded, filled, fill_out, ok, pe_ok, back, io, nat = (m.sem("gs_" + x) for x in (
        "loaded", "filled", "fill_out", "vector", "tensor", "back", "iota", "natural"))
    ring_ok, seen, nat_ok = m.token("scatter_ring"), m.token("scatter_seen"), m.token("natural_used")
    scattered = [m.sem(f"gs_sc{h}") for h in range(2)]
    rring = m.ring2[:].bitcast(I32)
    rec = m.rec_src.rearrange("(p t) w -> p t w", p=P)
    KN = -(-TD // P)
    nat_i = m.ring[:].rearrange("p r g n -> p (r g n)").bitcast(I32)[:, 0:KN * EP].rearrange("p (k l) -> p k l", l=EP)
    nat_f = m.oh[:].rearrange("p r g n -> p (r g n)")[:, 0:KN * EP].rearrange("p (k l) -> p k l", l=EP)
    place_tile = m.gi_s[:].bitcast(F32)
    pairs = [(c, k) for c in range(-(-T // P)) for k in (c - 1, c) if 0 <= k < KN]
    places = lambda c: slice(P * c, min(P * c + P, T))
    pick = lambda n: w.picks[:, P * n:P * n + places(pairs[n][0]).stop - places(pairs[n][0]).start]
    cut = (KN - 1) * P

    with nc.Block() as block:
        @block.sync
        def _(sp):
            sp.dma_start(w.key, m.a["src"].rearrange("(p c) -> p c", c=EC)).then_inc(loaded, 16)
            sp.dma_start(w.other, m.a["dst"].rearrange("(p c) -> p c", c=EC)).then_inc(loaded, 16)
            sp.wait_ge(filled, 1)
            for c in range(T // 16):
                sp.dma_start(rec[:, 16 * c:16 * c + 16, :], w.fill).then_inc(fill_out, 16)
            take(sp, nat_ok)
            for ends in (m.dst_g, m.src_g):
                sp.dma_start(nat_i[:, 0:KN - 1, :], ends[0:cut * EP].rearrange("(k p l) -> p k l", p=P, l=EP)).then_inc(nat, 16)
                sp.dma_start(nat_i[0:TD - cut, KN - 1, :], ends[cut * EP:E].rearrange("(p l) -> p l", l=EP)).then_inc(nat, 16)
                take(sp, nat_ok)
            for h in range(2):
                sp.wait_ge(scattered[h], 16 * G)
                sp.sem_inc(seen)
            with sp.Fori(1, NGE // 2) as i:
                for h in range(2):
                    sp.wait_ge(scattered[h], 16 * G * (i + 1))
                    sp.sem_inc(seen)
            sp.dma_start(w.back, rec).then_inc(back, 16)

        @block.gpsimd
        def _(pool):
            block_masks(m, pool, w, mask_free, mask_ready, m.token("numbered"))
            pool.wait_ge(fill_out, 16 * (T // 16))
            with pool.Fori(0, NGE // 2) as i:
                for h in range(2):
                    take(pool, ring_ok)
                    for j in range(G):
                        nc.gpsimd.indirect_dma_start(
                            out=m.rec_src, out_offset=bass.IndirectOffsetOnAxis(ap=m.idx[0:EP, h, j:j + 1], axis=0),
                            in_=rring[0:EP, h, j, 0:4], in_offset=None).then_inc(scattered[h], 16)
            nc.gpsimd.iota(w.iota_t, [[1, T]], base=0, channel_multiplier=0,
                           allow_small_or_imprecise_dtypes=True).then_inc(io, 1)

        @block.scalar
        def _(act):
            act.wait_ge(ok, 2)

            def fill_ring(g, h):
                nc.scalar.copy(m.idx[0:EP, h, :], w.row[:, bass.ds(g * G, G)])
                nc.scalar.copy(rring[0:EP, h, 0:G, 0:4], w.recs[:, bass.ds(g * G, G), :]).then_inc(ring_ok, 1)
            fill_ring(0, 0)
            fill_ring(1, 1)
            with act.Fori(1, NGE // 2) as i:
                for h in range(2):
                    take(act, seen)
                    fill_ring(2 * i + h, h)
            take(act, seen, 2)

        @block.tensor
        def _(pe):
            pe.wait_ge(ok, 1)
            nc.tensor.matmul(m.PS[:, 0, 0:NB], m.ones[0:EP, :], w.cnt[0:EP, :], start=True, stop=True)
            nc.tensor.matmul(m.PS[:, 1, 0:NB], m.tri[0:EP, :], w.cnt[0:EP, :], start=True, stop=True).then_inc(pe_ok, 1)
            for n in range(2):
                pe.wait_ge(ok, 3 + n)
                for i, (c, k) in enumerate(pairs):
                    at = slice(P * (c % 4), P * (c % 4) + places(c).stop - places(c).start)
                    t = nc.tensor.matmul(m.PS[0:EP, c // 4, at], nat_f[:, k, :], pick(i), start=k == max(c - 1, 0),
                                         stop=k == min(c, KN - 1))
                t.then_inc(pe_ok, 1)
            pe.wait_ge(ok, 5)
            nc.tensor.transpose(m.PS[0:NB, 4, 0:P], w.incl, m.ident[:]).then_inc(pe_ok, 1)
            pe.wait_ge(ok, 6)
            for k in range(4):
                t = nc.tensor.matmul(m.PS[0:1, k, 0:q], m.ones[0:NB, 0:1], w.cmp[:, q * k:q * k + q],
                                     start=True, stop=True)
            t.then_inc(pe_ok, 1)

        @block.vector
        def _(v):
            V = nc.vector
            step = steps(m, v, m.token("ch"))
            V.memset(w.fill[:, :, 2:4], 0)
            V.memset(w.fill[:, :, 0:1], NO_ROW)
            step(V.memset(w.fill[:, :, 1:2], NO_NODE))
            v.sem_inc(filled)
            step(V.memset(w.cnt, 0.0))
            step(V.memset(w.zero, 0.0))
            step(V.memset(w.none, 0.0))
            step(V.memset(nat_i[:, KN - 1, :], 0))
            v.sem_inc(nat_ok)
            v.wait_ge(loaded, 32)
            step(V.tensor_scalar(w.hi, w.key, 7, None, ALU.logical_shift_right))
            step(V.tensor_copy(w.blk, w.hi))
            count_blocks(m, v, w, counted, w.cnt)
            v.sem_inc(ok)
            v.wait_ge(pe_ok, 1)
            step(V.tensor_scalar(w.tiles, m.PS[:, 0, 0:NB], float(P - 1), None, ALU.add))
            step(V.tensor_copy(w.tiles_i, w.tiles))
            step(V.tensor_scalar(w.tiles_i, w.tiles_i, 7, None, ALU.logical_shift_right))
            step(V.tensor_copy(w.tiles, w.tiles_i))
            step(V.tensor_tensor_scan(w.incl, w.tiles, w.none, 0.0, ALU.add, ALU.add))
            step(V.tensor_tensor(w.base, w.incl, w.tiles, ALU.subtract))
            step(V.tensor_scalar(w.base, w.base, float(P), -1.0, ALU.mult, ALU.add))
            step(V.tensor_tensor(w.base, w.base, m.PS[:, 1, 0:NB], ALU.add))
            rank_edges(m, v, w, step, *turns)
            step(V.tensor_copy(w.row, w.pos))
            step(V.tensor_scalar(w.hi, w.row, 7, None, ALU.logical_shift_right))
            step(V.tensor_scalar(w.row, w.row, P - 1, None, ALU.bitwise_and))
            step(V.scalar_tensor_tensor(out=w.row, in0=w.row, scalar=float(T), in1=w.hi, op0=ALU.mult, op1=ALU.add))
            step(V.tensor_copy(w.recs[:, :, 0], w.other))
            step(V.tensor_scalar(w.recs[:, :, 1], w.key, P - 1, None, ALU.bitwise_and))
            step(V.tensor_copy(w.recs[:, :, 2], w.zero))
            step(V.tensor_copy(w.recs[:, :, 3], w.zero))
            v.sem_inc(ok)
            for i, (c, k) in enumerate(pairs):
                step(V.tensor_scalar(pick(i), place_tile[:, places(c)], float(-P * k), m.pidx[:], ALU.add, ALU.is_equal))
            for n in range(2):
                v.wait_ge(nat, 32 * (n + 1))
                step(V.tensor_copy(nat_f, nat_i))
                v.sem_inc(nat_ok)
                v.sem_inc(ok)
                v.wait_ge(pe_ok, 2 + n)
                for b in range(4):
                    at = slice(4 * P * b, min(4 * P * (b + 1), T))
                    got = m.PS[0:EP, b, 0:at.stop - at.start]
                    if n == 0:
                        step(V.tensor_tensor(m.li_d[0:EP, at], got, m.li_d[0:EP, at], ALU.subtract))
                    else:
                        step(V.tensor_copy(m.gi_d[0:EP, at], got))
            v.sem_inc(ok)
            v.wait_ge(pe_ok, 4)
            v.wait_ge(io, 1)
            step(V.tensor_copy(w.col[:, 0:1], m.PS[0:NB, 4, 0:1]))
            step(V.tensor_scalar(w.cmp, w.iota_t, w.col[:, 0:1], None, ALU.is_ge))
            v.sem_inc(ok)
            v.wait_ge(pe_ok, 5)
            of_tile = m.ring[:].rearrange("p r g n -> p (r g n)").bitcast(I32)[0:1, 0:T]
            for k in range(4):
                step(V.tensor_scalar(of_tile[:, q * k:q * k + q], m.PS[0:1, k, 0:q], float(NB - 1), None, ALU.min))
            pack_blocks(m, step, of_tile, m.bt_s)
            v.wait_ge(back, 16)
            step(V.tensor_copy(m.gi_s[:], w.back[:, :, 0]))
            step(V.tensor_copy(m.li_s[:], w.back[:, :, 1]))


def load_nodes(m):
    nc = m.nc
    z, ld = m.sem("x_zero"), m.sem("x_loaded")
    with nc.Block() as block:
        @block.vector
        def _(v):
            nc.vector.memset(m.X[:, NB - 1, :], 0.0).then_inc(z, 1)

        @block.sync
        def _(sp):
            full = (NB - 1) * P
            sp.dma_start(m.X[:, 0:NB - 1, :], m.a["x"][0:full, :].rearrange("(b p) d -> p b d", p=P)).then_inc(ld, 16)
            sp.wait_ge(z, 1)
            sp.dma_start(m.X[0:LAST, NB - 1, :], m.a["x"][full:N, :]).then_inc(ld, 16)
            sp.wait_ge(ld, 32)


def tile_offsets(m, eng, bt, g, row, start):
    word = eng.value_load(bt[0:1, bass.ds(g, 1)])
    offsets = []
    for j in range(G):
        block = m.nc.s_assert_within((word >> (7 * j)) & 127, 0, NB - 1,
                                     skip_runtime_bounds_check_because="the packed blocks are at most NB - 1")
        reg = eng.alloc_register()
        eng.reg_mov(reg, block * row + start)
        offsets.append(m.nc.s_assert_within(eng.snap(reg), start, (NB - 1) * row + start,
                                            skip_runtime_bounds_check_because="so is each one's offset"))
    return offsets


def edge_pass(m, tag, table, width, gi, li, bt, col, ncols, ones=False, attr=False, heads=0, weights=None):
    nc = m.nc
    got_attr = [m.sem(f"{tag}_attr{h}") for h in range(R)] if attr else None
    got = [m.sem(f"{tag}_got{h}") for h in range(R)]
    s = Parts()
    s.idx_ready = m.token("idx_ready")
    s.idx_free = m.token("idx_free")
    s.ring2_free = m.token("ring2_free")
    s.ring_free = m.token("ring_free")
    s.landed = m.token("landed")
    s.oh_ready = m.token("oh_ready")
    s.summed = m.token("summed")
    s.ps_free = m.token("ps_free")
    s.added = m.token("added")
    s.ohT_psum = m.token("ohT_psum")
    s.ohT_ready = m.token("ohT_ready")
    s.hs_ready = m.token("hs_ready")
    s.d_ready = m.token("d_ready")
    s.w_ready = m.token("w_ready")
    s.msg_ready = m.token("msg_ready")
    s.ch = m.token("ch")
    s.init = m.token("init")
    PM = lambda g, j: m.PS[:, 2 * (g % 2) + j // 2, RW * (j % 2):RW * (j % 2) + ncols]
    PT = lambda g: m.PS[:, 4 + g % 2, :].rearrange("p (j n) -> p j n", j=G)
    PH = lambda g: m.PS[:, 6 + g % 2, 0:8 * G].rearrange("p (j n) -> p j n", j=G)
    nh = heads

    def groups(eng, body):
        for h in range(R):
            body(h, h, 0)
        with eng.Fori(1, NG // R - 1) as i:
            for h in range(R):
                body(R * i + h, h, i)
        for h in range(R):
            body(NG - R + h, h, NG // R - 1)

    def exists(g):
        return not isinstance(g, int) or 0 <= g < NG

    with nc.Block() as block:
        @block.sync
        def _(sp):
            def body(g, h, i):
                sp.wait_ge(got[h], 16 * G * (i + 1))
                if attr:
                    sp.wait_ge(got_attr[h], 16 * G * (i + 1))
                sp.sem_inc(s.idx_free)
                sp.sem_inc(s.landed)
            groups(sp, body)

        @block.gpsimd
        def _(pool):
            def body(g, h, i):
                take(pool, s.idx_ready)
                if exists(g - R):
                    take(pool, s.ring_free)
                for j in range(G):
                    nc.gpsimd.indirect_dma_start(
                        out=m.ring[:, h, j, 0:width], out_offset=None, in_=table,
                        in_offset=bass.IndirectOffsetOnAxis(ap=m.idx[:, h, j:j + 1], axis=0)).then_inc(got[h], 16)
            groups(pool, body)
            take(pool, s.ring_free, R)

        @block.scalar
        def _(act):
            def indices(g, h):
                nc.scalar.copy(m.idx[:, h, :], gi[:, bass.ds(g * G, G)]).then_inc(s.idx_ready, 1)

            def features(source, g, h):
                for j in range(G):
                    t = act.value_load(m.tile_of[:, bass.ds(g * G + j, 1)], min_val=0, max_val=TD - 1)
                    act.dma_start(m.ring2[0:EP, h, j, :], source[bass.ds(t * EP, EP), :]).then_inc(got_attr[h], 16)

            def run(source):
                for g in range(R):
                    indices(g, g)
                    if attr:
                        features(source, g, g)
                if nh:
                    transposed(0)
                    transposed(1)
                    weigh(0, 0)

                def body(g, h, i):
                    if nh and exists(g + 2):
                        transposed(h + 2)
                    if nh and exists(g + 1):
                        weigh(g + 1, h + 1)
                    take(act, s.idx_free)
                    if exists(g + R):
                        indices(g + R, h)
                    if attr:
                        take(act, s.ring2_free)
                        if exists(g + R):
                            features(source, g + R, h)
                groups(act, body)

            def transposed(h):
                take(act, s.ohT_psum)
                nc.scalar.copy(m.ohT[:, h % 2], PT(h)).then_inc(s.ohT_ready, 1)

            def weigh(g, h):
                take(act, s.d_ready)
                nc.scalar.activation(m.ring[:, h % R, :, D:D + nh], m.dd[:, h % 2, :, 0:nh], ACT.Exp).then_inc(s.w_ready, 1)
                if nh == 2:
                    nc.scalar.activation(m.w1[:, bass.ds(g * G, G)], m.dd[:, h % 2, :, 1], ACT.Exp)

            if attr:
                take(act, s.ring2_free, R)
                unsorted = act.value_load(m.unsorted[:], min_val=0, max_val=1)
                with act.If_ne(act.to_reg(unsorted), 0):
                    run(m.attr_g)
                with act.Else():
                    run(m.a["edge_attr_128"])
                act.drain()
            else:
                run(None)

        @block.tensor
        def _(pe):
            take(pe, s.init)

            def turn(h):
                take(pe, s.oh_ready)
                for j in range(G):
                    t = nc.tensor.transpose(PT(h)[:, j, :], m.oh[:, h % R, j, :], m.ident[:])
                t.then_inc(s.ohT_psum, 1)

            own_scores = m.node[:].rearrange("p b n -> p (b n)")

            def scores(offsets, h):
                take(pe, s.ohT_ready)
                for j in range(G):
                    t = nc.tensor.matmul(PH(h)[:, j, 0:2 * nh], m.ohT[:, h % 2, j, :],
                                         own_scores[:, bass.ds(offsets[j], 2 * nh)],
                                         start=True, stop=True)
                t.then_inc(s.hs_ready, 1)
            if nh:
                for g in (0, 1):
                    turn(g)
                    scores(tile_offsets(m, pe, bt, g, 8, 0), g)

            def body(g, h, i):
                if nh and exists(g + 2):
                    turn(h + 2)
                    offsets = tile_offsets(m, pe, bt, g + 2, 8, 0)
                if not nh:
                    take(pe, s.oh_ready)
                if nh or weights is not None:
                    take(pe, s.msg_ready)
                else:
                    take(pe, s.landed)
                if exists(g - 2):
                    take(pe, s.ps_free)
                for j in range(G):
                    t = nc.tensor.matmul(PM(h, j), m.oh[:, h, j, :], m.ring[:, h, j, 0:ncols],
                                         start=True, stop=not attr)
                    if attr:
                        t = nc.tensor.matmul(PM(h, j), m.oh[:, h, j, :], m.ring2[:, h, j, :], start=False, stop=True)
                t.then_inc(s.summed, 1)
                if nh and exists(g + 2):
                    scores(offsets, h + 2)
            groups(pe, body)
            take(pe, s.ps_free, 2)

        @block.vector
        def _(v):
            V = nc.vector
            if ones:
                V.memset(m.ring[:, :, :, D:D + 1], 1.0)
            V.memset(m.rmax[:], -3e38)
            V.memset(m.A[:, :, col:col + ncols], 0.0).then_inc(s.ch, 1)
            take(v, s.ch)
            v.sem_inc(s.init)
            if attr:
                V.memset(m.ring2[:], 0.0).then_inc(s.ch, 1)
                take(v, s.ch)
                v.sem_inc(s.ring2_free, R)

            def one_hot(g, h):
                V.tensor_tensor(m.oh[:, h % R], bc(m.iota[:].unsqueeze(1), (P, G, P)),
                                bc(li[:, bass.ds(g * G, G)].unsqueeze(2), (P, G, P)), ALU.is_equal).then_inc(s.oh_ready, 1)

            sums = m.A[:].rearrange("p b w -> p (b w)")

            def add_up(offsets, h):
                take(v, s.summed)
                v.sem_inc(s.ring_free)
                if attr:
                    v.sem_inc(s.ring2_free)
                for j in range(G):
                    dst = sums[:, bass.ds(offsets[j], ncols)]
                    if j:
                        v.wait_ge(s.added, j)
                    V.tensor_tensor(dst, dst, PM(h, j), ALU.add).then_inc(s.added, 1)
                take(v, s.added, G)
                v.sem_inc(s.ps_free)

            def exponents(g, h):
                sc, lr, dd = (x[:, h % 2, :, 0:nh] for x in (m.sc, m.lr, m.dd))
                take(v, s.landed)
                take(v, s.hs_ready)
                V.tensor_tensor(sc, PH(h)[:, :, 0:nh], m.ring[:, h % R, :, D:D + nh], ALU.add).then_inc(s.ch, 1)
                v.wait_ge(s.ch, 1)
                V.scalar_tensor_tensor(out=lr, in0=sc, scalar=SLOPE, in1=sc, op0=ALU.mult, op1=ALU.max).then_inc(s.ch, 1)
                v.wait_ge(s.ch, 2)
                V.tensor_tensor(dd, lr, PH(h)[:, :, nh:2 * nh], ALU.subtract).then_inc(s.d_ready, 1)
                if nh == 4:
                    V.tensor_tensor(m.rmax[:], m.rmax[:], lr, ALU.max).then_inc(s.ch, 1)
                take(v, s.ch, 3 if nh == 4 else 2)

            one_hot(0, 0)
            one_hot(1, 1)
            if nh:
                exponents(0, 0)

            def body(g, h, i):
                if exists(g + 2):
                    one_hot(g + 2, h + 2)
                if nh:
                    take(v, s.w_ready)
                    rows = m.ring[:, h, :, 0:D].rearrange("p j (n d) -> p j n d", n=nh)
                    w = bc(m.ring[:, h, :, D:D + nh].unsqueeze(3), (P, G, nh, D // nh))
                    V.tensor_tensor(rows, rows, w, ALU.mult).then_inc(s.msg_ready, 1)
                if weights is not None:
                    take(v, s.landed)
                    rows = m.ring[:, h, :, 0:width]
                    V.tensor_tensor(rows, rows, bc(weights[:, bass.ds(g * G, G)].unsqueeze(2), (P, G, width)),
                                    ALU.mult).then_inc(s.msg_ready, 1)
                if exists(g - 1):
                    add_up(tile_offsets(m, v, bt, g - 1, RW, col), h - 1)
                if nh and exists(g + 1):
                    exponents(g + 1, h + 1)
            groups(v, body)
            add_up(tile_offsets(m, v, bt, NG - 1, RW, col), R - 1)


def chunks(eng, body):
    for h in range(2):
        body(h, h)
    with eng.Fori(1, NC // 2 - 1) as i:
        for h in range(2):
            body(2 * i + h, h)
    for h in range(2):
        body(NC - 2 + h, h)


def chunk_exists(c):
    return not isinstance(c, int) or 0 <= c < NC


def chunk(t, c, lo=0, hi=None):
    return t[:, bass.ds(c * CB, CB), lo:t.shape[2] if hi is None else hi]


def layer_norm(m, v, seq, dst, var_ready, std_ready):
    V = m.nc.vector
    mean, var, std, rstd = (m.st[:, k, :] for k in range(4))
    seq(V.tensor_reduce(mean, m.Y[:], AX, ALU.add))
    seq(V.tensor_scalar(mean, mean, -1.0 / D, None, ALU.mult))
    seq(V.tensor_tensor(m.Y[:], m.Y[:], bc(mean.unsqueeze(2), (P, CB, D)), ALU.add))
    seq(V.tensor_tensor(m.S[:], m.Y[:], m.Y[:], ALU.mult))
    seq(V.tensor_reduce(var, m.S[:], AX, ALU.add))
    V.tensor_scalar(var, var, 1.0 / D, EPS, ALU.mult, ALU.add).then_inc(var_ready, 1)
    take(v, std_ready)
    seq(V.reciprocal(rstd, std))
    return V.tensor_tensor(dst, m.Y[:], bc(rstd.unsqueeze(2), (P, CB, D)), ALU.mult)


def root(m, act, var_ready, std_ready):
    take(act, var_ready)
    m.nc.scalar.activation(m.st[:, 2, :], m.st[:, 1, :], ACT.Sqrt).then_inc(std_ready, 1)


def nodes_sage(m):
    nc = m.nc
    ch, mean_ok, tp, cp, mm, x_ok, vr, sr = (m.token(x) for x in (
        "ch", "mean", "transposed", "copied", "product", "x_ready", "var", "std"))
    o = m.sem("n0_stored")
    xc_ok = m.token("xc_ready")
    TP1 = m.PS[:, 0:2, :].rearrange("p k (j n) -> p (k j) n", j=4)
    TP2 = m.PS[:, 2:4, :].rearrange("p k (j n) -> p (k j) n", j=4)
    PO = [m.PS[:, 4 + 2 * h:6 + 2 * h, :].rearrange("p k (j n) -> p (k j) n", j=4) for h in range(2)]
    with nc.Block() as block:
        @block.vector
        def _(v):
            V = nc.vector
            seq = steps(m, v, ch)

            def mean(c, h):
                V.tensor_tensor(m.M2[h % 2], chunk(m.A, c, 0, D), bc(chunk(m.rec, c, 0, 1), (P, CB, D)),
                                ALU.mult).then_inc(mean_ok, 1)
            deg = m.rec[:, :, 0:1]
            seq(V.tensor_scalar(deg, m.A[:, :, D:D + 1], 1.0, None, ALU.max))
            seq(V.reciprocal(deg, deg))
            mean(0, 0)
            mean(1, 1)

            def body(c, h):
                if chunk_exists(c + 2):
                    mean(c + 2, h)
                seq(V.tensor_tensor(m.Y[:], PO[h][:, 0:CB, :], chunk(m.X, c), ALU.add))
                seq(layer_norm(m, v, seq, chunk(m.X, c), vr, sr))
                v.sem_inc(x_ok)

            def wait_then_body(c, h):
                take(v, mm)
                body(c, h)
            chunks(v, wait_then_body)

        @block.tensor
        def _(pe):
            def turn(h):
                take(pe, mean_ok)
                take(pe, xc_ok)
                for k in range(CB):
                    nc.tensor.transpose(TP1[:, k, :], m.xc2[h % 2][:, k, :], m.ident[:])
                    t = nc.tensor.transpose(TP2[:, k, :], m.M2[h % 2][:, k, :], m.ident[:])
                t.then_inc(tp, 1)
            turn(0)

            def body(c, h):
                take(pe, cp, 2)
                if chunk_exists(c + 1):
                    turn(h + 1)
                for k in range(CB):
                    nc.tensor.matmul(PO[h][:, k, :], m.xT2[h][:, k, :], m.w["self"][:], start=True, stop=False)
                    nc.tensor.matmul(PO[h][:, k, :], m.mT2[h][:, k, :], m.w["neigh"][:], start=False, stop=False)
                    t = nc.tensor.matmul(PO[h][:, k, :], m.ones[0:2, :], m.bias[:], start=False, stop=True)
                t.then_inc(mm, 1)
            chunks(pe, body)

        @block.scalar
        def _(act):
            def nodes(c, h):
                nc.scalar.copy(m.xc2[h % 2], chunk(m.X, c)).then_inc(xc_ok, 1)

            def turned(h):
                take(act, tp)
                nc.scalar.copy(m.xT2[h % 2], TP1[:, 0:CB, :]).then_inc(cp, 1)
                nc.scalar.copy(m.mT2[h % 2], TP2[:, 0:CB, :]).then_inc(cp, 1)
            nodes(0, 0)
            nodes(1, 1)
            turned(0)

            def body(c, h):
                if chunk_exists(c + 1):
                    turned(h + 1)
                if chunk_exists(c + 2):
                    nodes(c + 2, h)
                root(m, act, vr, sr)
            chunks(act, body)

        @block.sync
        def _(sp):
            rows = m.tab1.rearrange("(b p) d -> p b d", p=P)
            with sp.Fori(0, NC) as c:
                take(sp, x_ok)
                sp.dma_start(rows[:, bass.ds(c * CB, CB), :], chunk(m.X, c)).then_inc(o, 16)
            sp.wait_ge(o, 16 * NC)


def nodes_project(m, tag, w, wa, nh, table, width, after_attention):
    nc = m.nc
    ch, x_ok, tp, cp, mm, h_ok, sc_ok, vr, sr, er, ed, mx, mxd, rows_free = (m.token(x) for x in (
        "ch", "x_ready", "transposed", "copied", "product", "h_ready", "sc_ready",
        "var", "std", "elu_in", "elu_out", "max_in", "max_out", "rows_free"))
    o = m.sem(tag + "_stored")
    TP1 = m.PS[:, 0:2, :].rearrange("p k (j n) -> p (k j) n", j=4)
    PO = [m.PS[:, 2 + 2 * h:4 + 2 * h, :].rearrange("p k (j n) -> p (k j) n", j=4) for h in range(2)]
    PSC = [m.PS[:, 6 + h, 0:8 * CB].rearrange("p (j n) -> p j n", j=CB) for h in range(2)]
    with nc.Block() as block:
        @block.vector
        def _(v):
            V = nc.vector

            def seq(ins):
                ins.then_inc(ch, 1)
                take(v, ch)
            if after_attention:
                seq(V.tensor_reduce(m.gmax[:, 0:1], m.rmax[:].rearrange("p a b -> p (a b)"), AX, ALU.max))
                V.memset(m.tmp4[:], 0.0).then_inc(mx, 1)
                take(v, mxd)
                seq(V.tensor_scalar(m.tmp4[:], m.node[:, :, 4:8], m.gmax[:, 1:2], -1.0, ALU.subtract, ALU.mult))
                V.tensor_scalar(m.tmp4[:], m.tmp4[:], 0.0, None, ALU.add).then_inc(er, 1)
                take(v, ed)
                seq(V.scalar_tensor_tensor(out=m.rec[:], in0=m.tmp4[:], scalar=1e-8, in1=m.A[:, :, D:D + 4],
                                           op0=ALU.mult, op1=ALU.add))
                seq(V.reciprocal(m.rec[:], m.rec[:]))
            def scores(c, h):
                take(v, mm)
                seq(V.tensor_copy(chunk(m.nbr, c, 0, nh), PSC[h % 2][:, :, 0:nh]))
                seq(V.tensor_copy(chunk(m.node, c, 0, nh), PSC[h % 2][:, :, nh:2 * nh]))
                v.sem_inc(sc_ok)

            def body(c, h):
                x = chunk(m.X, c)
                if after_attention:
                    for j in range(4):
                        seq(V.tensor_tensor(m.M[:, :, 32 * j:32 * j + 32], chunk(m.A, c, 32 * j, 32 * j + 32),
                                            bc(chunk(m.rec, c, j, j + 1), (P, CB, 32)), ALU.mult))
                    V.tensor_scalar(m.S[:], m.M, 0.0, None, ALU.min).then_inc(er, 1)
                    take(v, ed)
                    seq(V.scalar_tensor_tensor(out=m.Y[:], in0=m.M, scalar=0.0, in1=m.S[:], op0=ALU.max, op1=ALU.add))
                    seq(V.scalar_tensor_tensor(out=m.Y[:], in0=m.Y[:], scalar=-1.0, in1=x, op0=ALU.add, op1=ALU.add))
                else:
                    seq(V.scalar_tensor_tensor(out=m.Y[:], in0=x, scalar=2.0, in1=chunk(m.A, c, 0, D),
                                               op0=ALU.mult, op1=ALU.add))
                seq(layer_norm(m, v, seq, m.mT2[h], vr, sr))
                v.sem_inc(x_ok)
                if chunk_exists(c - 1):
                    scores(c - 1, h - 1)
            chunks(v, body)
            scores(NC - 1, 1)
            for j in range(nh):
                seq(V.tensor_reduce(m.gmax[:, j:j + 1], m.nbr[:, :, j], AX, ALU.max))
            v.sem_inc(mx)
            take(v, mxd)
            for j in range(nh):
                own, shift = m.node[:, :, j:j + 1], m.node[:, :, nh + j:nh + j + 1]
                seq(V.tensor_scalar(shift, own, m.sc[:, 0, 0, j:j + 1], None, ALU.add))
                seq(V.scalar_tensor_tensor(out=shift, in0=shift, scalar=SLOPE, in1=shift, op0=ALU.mult, op1=ALU.max))

        @block.gpsimd
        def _(pool):
            if after_attention:
                take(pool, mx)
                nc.gpsimd.partition_all_reduce(m.gmax[:, 1:2], m.gmax[:, 0:1], P, RMAX).then_inc(mxd, 1)
            take(pool, mx)
            nc.gpsimd.partition_all_reduce(m.sc[:, 0, 0, 0:nh], m.gmax[:, 0:nh], P, RMAX).then_inc(mxd, 1)

        @block.tensor
        def _(pe):
            def body(c, h):
                take(pe, x_ok)
                for k in range(CB):
                    t = nc.tensor.transpose(TP1[:, k, :], m.mT2[h][:, k, :], m.ident[:])
                t.then_inc(tp, 1)
                take(pe, cp, 2)
                for k in range(CB):
                    nc.tensor.matmul(PO[h][:, k, :], m.xT[:, k, :], w[:], start=True, stop=True)
                    t = nc.tensor.matmul(PSC[h][:, k, 0:2 * nh], m.xT[:, k, :], wa[:], start=True, stop=True)
                t.then_inc(h_ok, 1)
            chunks(pe, body)

        @block.scalar
        def _(act):
            if after_attention:
                take(act, er)
                nc.scalar.activation(m.tmp4[:], m.tmp4[:], ACT.Exp).then_inc(ed, 1)

            def rows_out(c, h):
                take(act, rows_free)
                take(act, h_ok)
                nc.scalar.copy(m.HR[:, h % 2, :, 0:D], PO[h % 2][:, 0:CB, :])
                nc.scalar.copy(m.HR[:, h % 2, :, D:D + nh], PSC[h % 2][:, :, 0:nh]).then_inc(mm, 1)

            def body(c, h):
                if chunk_exists(c - 1):
                    rows_out(c - 1, h - 1)
                if after_attention:
                    take(act, er)
                    nc.scalar.activation(m.S[:], m.S[:], ACT.Exp).then_inc(ed, 1)
                root(m, act, vr, sr)
                take(act, tp)
                nc.scalar.copy(m.xT, TP1[:, 0:CB, :]).then_inc(cp, 1)
                nc.scalar.copy(chunk(m.X, c), m.mT2[h]).then_inc(cp, 1)
            chunks(act, body)
            rows_out(NC - 1, 1)
            take(act, rows_free, 2)

        @block.sync
        def _(sp):
            rows = table.rearrange("(b p) d -> p b d", p=P)

            def body(c, h):
                take(sp, sc_ok)
                sp.dma_start(rows[:, bass.ds(c * CB, CB), :], m.HR[:, h, :, 0:width]).then_inc(o, 16)
                sp.wait_ge(o, 16 * (c + 1))
                sp.sem_inc(rows_free)
            sp.sem_inc(rows_free, 2)
            chunks(sp, body)
            sp.dma_start(table[NO_ROW:NO_ROW + 1, D:D + nh], m.low[:, 0:nh]).then_inc(o, 16)
            sp.wait_ge(o, 16 * (NC + 1))


def nodes_hop(m):
    nc = m.nc
    ch, ok, o = m.token("ch"), m.sem("n3_rows_ready"), m.sem("n3_stored")
    with nc.Block() as block:
        @block.vector
        def _(v):
            V = nc.vector

            def seq(ins):
                ins.then_inc(ch, 1)
                take(v, ch)
            den, r, t, u = m.A[:, :, D:D + 2], m.rec[:, :, 0:2], m.tmp4[:, :, 0:2], m.tmp4[:, :, 2:4]
            seq(V.tensor_scalar(t, den, 0.0, None, ALU.is_equal))
            seq(V.tensor_tensor(t, t, den, ALU.add))
            seq(V.reciprocal(r, t))
            seq(V.tensor_tensor(t, r, den, ALU.mult))
            seq(V.tensor_scalar(u, t, 0.0, None, ALU.is_equal))
            seq(V.tensor_tensor(u, u, t, ALU.add))
            seq(V.reciprocal(u, u))
            seq(V.tensor_tensor(r, r, u, ALU.mult))
            for i in (1, 0):
                rows = m.A[:, :, 64 * i:64 * i + 64]
                V.tensor_tensor(rows, rows, bc(m.rec[:, :, i:i + 1], (P, NB, 64)), ALU.mult).then_inc(ok, 1)

        @block.sync
        def _(sp):
            sp.wait_ge(ok, 1)
            sp.dma_start(m.tab4.rearrange("(b p) d -> p b d", p=P), m.A[:, :, 64:128]).then_inc(o, 16)
            sp.wait_ge(o, 16)


def nodes_final(m):
    nc = m.nc
    ch, gi_, go, ok, vr, sr = (m.token(x) for x in ("ch", "elu_in", "elu_out", "x_ready", "var", "std"))
    o = m.sem("n4_stored")
    with nc.Block() as block:
        @block.vector
        def _(v):
            V = nc.vector

            def seq(ins):
                ins.then_inc(ch, 1)
                take(v, ch)
            full = (P, CB, D)
            with v.Fori(0, NC) as c:
                seq(V.tensor_scalar(m.Y[:, :, 0:64], chunk(m.A, c, 0, 64), 0.0, None, ALU.add))
                seq(V.tensor_tensor(m.Y[:, :, 64:128], chunk(m.A, c, 64, 128), bc(chunk(m.rec, c, 1, 2), (P, CB, 64)), ALU.mult))
                seq(V.tensor_tensor(m.xT.bitcast(I32), m.Y[:], m.Y[:], ALU.is_equal))
                seq(V.memset(m.M, 0.0))
                seq(V.copy_predicated(m.M, m.xT.bitcast(I32), m.Y[:]))
                seq(V.tensor_tensor(m.M, m.M, bc(m.w["b3"][:].unsqueeze(1), full), ALU.add))
                seq(V.tensor_tensor(m.S[:], m.M, bc(m.w["fc3"][:].unsqueeze(1), full), ALU.mult))
                seq(V.tensor_reduce(m.gg[:], m.S[:].rearrange("p b (i d) -> p b i d", i=2), AX, ALU.add))
                V.tensor_tensor(m.gg[:], m.gg[:], bc(m.bf3[:].unsqueeze(1), (P, CB, 2)), ALU.add).then_inc(gi_, 1)
                take(v, go)
                seq(V.tensor_scalar(m.gg[:], m.gg[:], 1.0, None, ALU.add))
                seq(V.reciprocal(m.gg[:], m.gg[:]))
                seq(V.tensor_scalar(m.S[:], m.M, 0.0, None, ALU.min))
                for i in range(2):
                    h = m.S[:, :, 64 * i:64 * i + 64]
                    seq(V.tensor_tensor(h, h, bc(m.gg[:, :, i:i + 1], (P, CB, 64)), ALU.mult))
                seq(V.scalar_tensor_tensor(out=m.M, in0=m.M, scalar=0.0, in1=m.S[:], op0=ALU.max, op1=ALU.add))
                seq(V.scalar_tensor_tensor(out=m.M, in0=m.M, scalar=SLOPE, in1=m.M, op0=ALU.mult, op1=ALU.max))
                seq(V.tensor_tensor(m.Y[:], m.M, chunk(m.X, c), ALU.add))
                seq(layer_norm(m, v, seq, chunk(m.X, c), vr, sr))
                v.sem_inc(ok)

        @block.scalar
        def _(act):
            with act.Fori(0, NC) as c:
                take(act, gi_)
                nc.scalar.activation(m.gg[:], m.gg[:], ACT.Exp, scale=-1.0).then_inc(go, 1)
                root(m, act, vr, sr)

        @block.sync
        def _(sp):
            full = (NB - 1) * P
            rows = m.out[0:full, :].rearrange("(b p) d -> p b d", p=P)
            with sp.Fori(0, NC - 1) as c:
                take(sp, ok)
                sp.dma_start(rows[:, bass.ds(c * CB, CB), :], chunk(m.X, c)).then_inc(o, 16)
            take(sp, ok)
            b = (NC - 1) * CB
            sp.dma_start(rows[:, b:NB - 1, :], m.X[:, b:NB - 1, :]).then_inc(o, 16)
            sp.dma_start(m.out[full:N, :], m.X[0:LAST, NB - 1, :]).then_inc(o, 16)
            sp.wait_ge(o, 16 * (NC + 1))


NAMES = ["x", "src", "dst", "edge_attr_128", "L0_gnn_W_self", "L0_gnn_b_self", "L0_gnn_W_neigh", "L0_gnn_b_neigh",
         "L2_gnn_W", "L2_gnn_A_left", "L2_gnn_A_right", "L3_gnn_W", "L3_gnn_b", "L3_gnn_fc", "L3_gnn_bf",
         "L3_gnn_a_src", "L3_gnn_a_dst"]


def kernel(**inputs):
    import numpy as np
    import concourse.bacc as bacc
    from concourse.bass_utils import run_bass_kernel_spmd

    nc = bacc.Bacc("TRN2", target_bir_lowering=False, num_devices=1)
    arrays, aps = {}, {}
    for name in NAMES:
        arr = np.ascontiguousarray(inputs[name])
        arrays["in_" + name] = arr
        aps[name] = nc.dram_tensor("in_" + name, arr.shape, mybir.dt.from_np(arr.dtype), kind="ExternalInput").ap()
    out = nc.dram_tensor("out_0", (N, D), F32, kind="ExternalOutput").ap()
    build(nc, aps, out)
    r = run_bass_kernel_spmd(nc, [arrays], core_ids=[0])
    return r.results[0]["out_0"]
```
